# Optimizing a Trainium2 kernel written in Bass

```python
import numpy as np
import jax
import jax.numpy as jnp

def _softmax(x, axis=-1):
    return jax.nn.softmax(x, axis=axis)

def _gelu(x):
    return jax.nn.gelu(x, approximate=True)

def _silu(x):
    return jax.nn.silu(x)

def _sigmoid(x):
    return jax.nn.sigmoid(x)

def _layernorm(x, axis=-1, eps=1e-05):
    m = jnp.mean(x, axis=axis, keepdims=True)
    v = jnp.var(x, axis=axis, keepdims=True)
    return (x - m) / jnp.sqrt(v + eps)

def _scatter_add(tgt, idx, src, axis=0):
    return tgt.at[idx].add(src)

def _segment_sum(src, seg, n):
    return jax.ops.segment_sum(src, seg, n)
kernel_name = 'mk_metaformer_d1_conv_nhwc512_r4_25d84a'

def setup_inputs(seed: int=0):
    np.random.seed(seed)
    _w = jnp.asarray

    def _rec_inputs():
        import jax
        import jax.numpy as jnp
        _gk = jax.random.key(seed)
        x = -0.0001538 + 1 * jax.random.normal(jax.random.fold_in(_gk, 1), (16, 16, 48, 128), jnp.float32)
        return x
    x = _rec_inputs()

    def _L0_conv_setup():
        import jax, jax.numpy as jnp
        import numpy as np
        import math
        H = 8
        MAX_POS = 48
        MAX_PART = 16

        def _rel_bias(table, L, max_len):
            b = table[max_len - L:max_len + L - 1]
            idx = jnp.arange(L)
            rel = idx[None, :] - idx[:, None] + (L - 1)
            return jnp.transpose(b[rel], (2, 0, 1))
        key = jax.random.key(seed)
        ks = jax.random.split(key, 7)
        B, N, T, C = (16, 16, 48, 128)
        s = 0.02
        return {'x': jax.random.normal(ks[0], (B, N, T, C), jnp.float32), 'Wq': jax.random.normal(ks[1], (C, C), jnp.float32) * s, 'Wk': jax.random.normal(ks[2], (C, C), jnp.float32) * s, 'Wv': jax.random.normal(ks[3], (C, C), jnp.float32) * s, 'Wo': jax.random.normal(ks[4], (C, C), jnp.float32) * s, 'rel_pos_bias': jax.random.normal(ks[5], (2 * MAX_POS - 1, H), jnp.float32) * s, 'particle_rel_pos_bias': jax.random.normal(ks[6], (2 * MAX_PART - 1, H), jnp.float32) * s}
    _L0_conv_all = _L0_conv_setup()
    _L0_conv_in = {k: v for k, v in _L0_conv_all.items() if k in ('Wq', 'Wk', 'Wv', 'Wo', 'rel_pos_bias', 'particle_rel_pos_bias')}
    del _L0_conv_all

    def _L0_ffn_setup():
        import jax, jax.numpy as jnp
        import numpy as np
        K = 2
        key = jax.random.key(seed)
        ks = jax.random.split(key, 6)
        B, T, d, E, dff = (2, 512, 128, 8, 512)
        x = jax.random.normal(ks[0], (B, T, d), dtype=jnp.float32)
        Wg = jax.random.normal(ks[1], (d, E), dtype=jnp.float32) * 0.02
        W1 = jax.random.normal(ks[2], (E, d, dff), dtype=jnp.float32) * 0.02
        b1 = jnp.zeros((E, dff), dtype=jnp.float32)
        W2 = jax.random.normal(ks[3], (E, dff, d), dtype=jnp.float32) * 0.02
        b2 = jnp.zeros((E, d), dtype=jnp.float32)
        return {'x': x, 'Wg': Wg, 'W1': W1, 'b1': b1, 'W2': W2, 'b2': b2}
    _L0_ffn_all = _L0_ffn_setup()
    _L0_ffn_in = {k: v for k, v in _L0_ffn_all.items() if k in ('Wg', 'W1', 'b1', 'W2', 'b2')}
    del _L0_ffn_all
    return {'x': x, 'L0_conv_Wq': _L0_conv_in['Wq'], 'L0_conv_Wk': _L0_conv_in['Wk'], 'L0_conv_Wv': _L0_conv_in['Wv'], 'L0_conv_Wo': _L0_conv_in['Wo'], 'L0_conv_rel_pos_bias': _L0_conv_in['rel_pos_bias'], 'L0_conv_particle_rel_pos_bias': _L0_conv_in['particle_rel_pos_bias'], 'L0_ffn_Wg': _L0_ffn_in['Wg'], 'L0_ffn_W1': _L0_ffn_in['W1'], 'L0_ffn_b1': _L0_ffn_in['b1'], 'L0_ffn_W2': _L0_ffn_in['W2'], 'L0_ffn_b2': _L0_ffn_in['b2']}

def reference(x, L0_conv_Wq, L0_conv_Wk, L0_conv_Wv, L0_conv_Wo, L0_conv_rel_pos_bias, L0_conv_particle_rel_pos_bias, L0_ffn_Wg, L0_ffn_W1, L0_ffn_b1, L0_ffn_W2, L0_ffn_b2):
    import jax
    import jax.numpy as jnp

    def _L0_conv_ref(x, Wq, Wk, Wv, Wo, rel_pos_bias, particle_rel_pos_bias):
        import jax, jax.numpy as jnp
        import numpy as np
        import math
        H = 8
        MAX_POS = 48
        MAX_PART = 16

        def _rel_bias(table, L, max_len):
            b = table[max_len - L:max_len + L - 1]
            idx = jnp.arange(L)
            rel = idx[None, :] - idx[:, None] + (L - 1)
            return jnp.transpose(b[rel], (2, 0, 1))
        B, N, T, C = x.shape
        hd = C // H
        L = N * T
        xf = x.reshape(B, L, C)
        q = (xf @ Wq).reshape(B, L, H, hd).transpose(0, 2, 1, 3)
        k = (xf @ Wk).reshape(B, L, H, hd).transpose(0, 2, 1, 3)
        v = (xf @ Wv).reshape(B, L, H, hd).transpose(0, 2, 1, 3)
        att = jnp.einsum('bhqd,bhkd->bhqk', q, k) * (1.0 / math.sqrt(hd))
        att = att.reshape(B, H, N, T, N, T)
        bias_t = _rel_bias(rel_pos_bias, T, MAX_POS).reshape(1, H, 1, T, 1, T)
        bias_p = _rel_bias(particle_rel_pos_bias, N, MAX_PART).reshape(1, H, N, 1, N, 1)
        att = att + bias_t + bias_p
        causal = jnp.tril(jnp.ones((T, T), dtype=bool))
        att = jnp.where(causal[None, None, None, :, None, :], att, -jnp.inf)
        att = jax.nn.softmax(att.reshape(B, H, L, L), axis=-1)
        y = att @ v
        y = y.transpose(0, 2, 1, 3).reshape(B, L, C) @ Wo
        return y.reshape(B, N, T, C)

    def _L0_ffn_ref(x, Wg, W1, b1, W2, b2):
        import jax, jax.numpy as jnp
        import numpy as np
        K = 2
        logits = jnp.einsum('btd,de->bte', x, Wg)
        probs = jax.nn.softmax(logits, axis=-1)
        top_p, _top_i = jax.lax.top_k(probs, K)
        top_p = top_p / jnp.sum(top_p, axis=-1, keepdims=True)
        b2_sum = jnp.sum(b2, axis=0)
        out = jnp.zeros_like(x)
        for i in range(K):
            w_in = x * top_p[..., i:i + 1]
            h = jax.nn.gelu(jnp.einsum('btd,edf->ebtf', w_in, W1) + b1[:, None, None, :], approximate=False)
            out = out + jnp.einsum('ebtf,efd->btd', h, W2) + b2_sum
        return out

    def _gn(v, G=32, eps=1e-05):
        B_, H_, W_, C_ = v.shape
        g = v.reshape(B_, H_, W_, G, C_ // G)
        m = jnp.mean(g, axis=(1, 2, 4), keepdims=True)
        s = jnp.var(g, axis=(1, 2, 4), keepdims=True)
        return ((g - m) / jnp.sqrt(s + eps)).reshape(v.shape)

    def _ln_c(v, eps=1e-06):
        m = jnp.mean(v, axis=-1, keepdims=True)
        s = jnp.var(v, axis=-1, keepdims=True)
        return (v - m) / jnp.sqrt(s + eps)

    def _ln_t(v, eps=1e-05):
        m = jnp.mean(v, axis=-1, keepdims=True)
        s = jnp.var(v, axis=-1, keepdims=True)
        return (v - m) / jnp.sqrt(s + eps)

    def _to_tokens(v):
        B_, H_, W_, C_ = v.shape
        return v.reshape(B_, H_ * W_, C_)

    def _from_tokens(t, like):
        return t.reshape(like.shape)
    x = x + _L0_conv_ref(_ln_c(x), L0_conv_Wq, L0_conv_Wk, L0_conv_Wv, L0_conv_Wo, L0_conv_rel_pos_bias, L0_conv_particle_rel_pos_bias)
    t = _to_tokens(x)
    t = t + _L0_ffn_ref(_ln_t(t), L0_ffn_Wg, L0_ffn_W1, L0_ffn_b1, L0_ffn_W2, L0_ffn_b2)
    x = _from_tokens(t, x)
    return x

_drawn_inputs = setup_inputs


def setup_inputs(seed=0):
    import zlib

    import numpy as np

    out = dict(_drawn_inputs(seed))
    spreads = {'L0_ffn_b1': (0.0, 0.1), 'L0_ffn_b2': (0.0, 0.1)}
    factors = {'L0_conv_Wq': 8.0,
     'L0_conv_Wk': 8.0,
     'L0_conv_Wv': 8.0,
     'L0_conv_Wo': 8.0,
     'L0_conv_rel_pos_bias': 8.0,
     'L0_conv_particle_rel_pos_bias': 8.0,
     'L0_ffn_Wg': 8.0}
    for name, (base, spread) in spreads.items():
        noise = np.random.default_rng([zlib.crc32(name.encode()), seed]).standard_normal(out[name].shape)
        drawn = base * np.exp(spread * noise) if base else spread * noise
        out[name] = jnp.asarray(drawn.astype(out[name].dtype))
    for name, factor in factors.items():
        out[name] = (out[name] * factor).astype(out[name].dtype)
    return out
```

```python
from contextlib import ExitStack

import concourse.bass as bass
from concourse import mybir

F32 = mybir.dt.float32
F32R = mybir.dt.float32r
BF16 = mybir.dt.bfloat16
I32 = mybir.dt.int32
ALU = mybir.AluOpType
ACT = mybir.ActivationFunctionType
AX = mybir.AxisListType

P = 128
BATCHES, PARTS, TIMES, C = 16, 16, 48, 128
HEADS, HD = 8, 16
TOK = PARTS * TIMES
TPT = P // PARTS
TILES = TOK // P
GH = 4
GROUPS = HEADS // GH
EXPERTS, DFF = 8, 512
FT = DFF // P
UNITS_PER_CHUNK = EXPERTS * FT
CHUNKS = 2
CT = TOK // CHUNKS
HT = TILES // CHUNKS
UNITS = CHUNKS * UNITS_PER_CHUNK
LAG = 4
NHS = 4
QCOLS = 512
ZW = 2688
NEG = -1e30
LN_EPS = (1e-6, 1e-5)
RSQRT_SEED = 1597463007.0
NEWTON = 3

Z_AT = {(0, 0): 0, (1, 0): 512, (2, 0): 896, (4, 1): 1152, (3, 0): 1408, (5, 1): 1536,
        (3, 1): 1664, (2, 1): 1920, (1, 1): 2176, (0, 1): 2432}


def attention_plan():
    plan = [(2, "norm", 0), (4, "turn", 0), (5, "query", 0), (6, "key", 0), (6, "value", 0)]
    plan += [(7, "stack", (0, hh)) for hh in range(GH)]
    plan += [(9 + n // 2, "maxima", (0, n // 3, n % 3)) for n in range(12)]
    plan += [(15, "rows", 0)]
    for hh in range(GH):
        plan += [(17 + (3 * hh + n) // 2, "scores", (0, hh, n)) for n in range(3)]
        plan += [(17 + (3 * hh + 2) // 2, "stack", (1, hh))]
    plan += [(24, "exp", 0)]
    plan += [(24, "maxima", (1, n // 3, n % 3)) for n in range(12)]
    plan += [(26, "mix", (0, 0)), (27, "divide", (0, 0)), (28, "mix", (0, 1)), (29, "divide", (0, 1))]
    plan += [(30, "rows", 1)]
    plan += [(32 + n, "scores", (1, n // 3, n % 3)) for n in range(12)]
    plan += [(45, "exp", 1), (47, "mix", (1, 0)), (48, "divide", (1, 0)), (49, "mix", (1, 1)),
             (50, "divide", (1, 1)), (51, "project", 0), (52, "norm", 1), (54, "turn", 1),
             (55, "gate", 0), (58, "split", 0), (60, "split", 1)]
    return plan


PLAN = attention_plan()
WIDE_STEPS = ("turn", "query", "key", "value", "maxima", "rows", "scores", "divide", "project", "split")
NARROW_STEPS = ("mix", "gate")
WIDE = {(s, a): n for n, (s, a) in enumerate([(s, a) for _, s, a in PLAN if s in WIDE_STEPS])}
NARROW = {(s, a): n for n, (s, a) in enumerate([(s, a) for _, s, a in PLAN if s in NARROW_STEPS])}
assert len(WIDE) % 2 == 0
WPB = len(WIDE) // 2
NPB = len(NARROW)
VCHAIN = 2 * 4 + 4 + 7


class Round:

    def __init__(self, eng, b):
        self.eng, self.b, self.base = eng, b, {}

    def at(self, per, n):
        if isinstance(self.b, int):
            return per * self.b + n
        if per not in self.base:
            self.base[per] = self.eng.snap(self.b * per)
        return self.base[per] + n


def window(ap, offset, dims):
    return bass.AP(ap.tensor, ap.offset + offset, [list(ap.ap[0])] + [list(d) for d in dims])


def build(nc, x, Wq, Wk, Wv, Wo, time_bias, part_bias, Wg, W1, b1, W2, b2, out):
    with ExitStack() as ctx:
        def sb(name, shape, dt=F32):
            return ctx.enter_context(nc.sbuf_tensor(name, shape, dt))

        def ps(name, shape):
            return ctx.enter_context(nc.psum_tensor(name, shape, F32))

        def sem(name):
            return ctx.enter_context(nc.semaphore(name))

        w1_hi = sb("w1_hi", [P, EXPERTS, DFF], F32R)
        w1_lo = sb("w1_lo", [P, EXPERTS, DFF], F32R)
        w2 = sb("w2", [P, EXPERTS * FT, C])
        b1_col = sb("b1_col", [P, EXPERTS * FT])
        b2_row = sb("b2_row", [P, C])
        wqkv = sb("wqkv", [P, 3, C])
        wo_pad = sb("wo_pad", [P, GROUPS, C])
        wg = sb("wg", [P, EXPERTS])
        ident = sb("ident", [P, P])
        spread = sb("spread", [P, P])
        key_table = sb("key_table", [P, HEADS, TOK])
        query_table = sb("query_table", [P, HEADS, TOK], BF16)
        xs = sb("xs", [P, TILES, C])
        xn = sb("xn", [P, TILES, C])
        act_t = sb("act_t", [P, TOK])
        halves = sb("halves", [P, 4, TOK])
        mixed = halves[:, 0, :]
        mixed_n = halves[:, 1:3, :]
        val = sb("val", [P, TILES, HEADS, 2 * HD])
        qst = sb("qst", [66, GH, TOK], F32R)
        kst = sb("kst", [66, GH, TOK], F32R)
        z = sb("z", [P, GH, ZW])
        maxes = sb("maxes", [P, GH * TILES])
        max_rows = act_t[0:GH * TILES, 512:TOK].rearrange("p (s t) -> p s t", s=2)
        stats = sb("stats", [P, TILES, 6])
        moments = sb("moments", [P, TILES, 2])
        ln_v = sb("ln_v", [P, TILES])
        ln_i = sb("ln_i", [P, TILES], I32)
        ln_y = sb("ln_y", [P, TILES])
        ln_t = sb("ln_t", [P, TILES])
        recip = halves[:, 3, 0:QCOLS]
        sorted_l, shifted, gate_e = (halves[:, 3, QCOLS + 48 * n:QCOLS + 48 * (n + 1)].rearrange(
            "p (i e) -> p i e", e=EXPERTS) for n in range(3))
        gate_s = sb("gate_s", [P, TILES, 4])
        probs = sb("probs", [P, TILES, 2])
        top = sb("top", [P, TILES, 2])
        ratio = sb("ratio", [P, TILES, 2])
        x0_hi = sb("x0_hi", [P, TOK], F32R)
        x0_lo = sb("x0_lo", [P, TOK], F32R)
        ratio_b = sb("ratio_b", [P, TOK])
        res = sb("res", [P, TILES, C])
        h0 = sb("h0", [P, 2, CT])
        h1 = sb("h1", [P, 2, CT])
        hsum = sb("hsum", [P, NHS, CT])
        outt = sb("outt", [P, HT, C])

        wide = [ps("wide0", [P, 1024]), ps("wide1", [P, 1024])]
        zps = [ps("zps0", [P, 512]), ps("zps1", [P, 512])]
        acc = ps("acc", [P, 512])
        narrow = ps("narrow", [P, 512])

        w1_stage = z[:, 0, 0:2048], z[:, 1, 0:2048]
        one_hot = [z[0:48, 2, 0:128], z[0:48, 2, 128:256]]
        t_stage = z[0:8, 2, 256:256 + 48 * 8]
        p_stage = z[32:48, 2, 256:256 + 16 * 8]
        b2_stage = z[0:8, 2, 768:896]
        twos = z[0:8, 2, 896:1024]
        b1_stage = z[0:32, 2, 1024:1152]
        rel = z[0:48, 3, 0:TOK]

        weights_loaded = sem("weights_loaded")
        w1_loaded = sem("w1_loaded")
        pool_set = sem("pool_set")
        vec_set = sem("vec_set")
        rel_ready = sem("rel_ready")
        table_filled = sem("table_filled")
        table_used = sem("table_used")
        setup_filled = sem("setup_filled")
        setup_done = sem("setup_done")
        act_set = sem("act_set")

        vec_met = sem("vec_met")
        pool_met = sem("pool_met")
        x_loaded = sem("x_loaded")
        vec_chain = sem("vec_chain")
        pool_chain = sem("pool_chain")
        ln_seeded = sem("ln_seeded")
        ln_rooted = sem("ln_rooted")
        xn_ready = sem("xn_ready")
        high_ready = sem("high_ready")
        stack_loaded = [sem(f"stack_loaded{n}") for n in range(GH)]
        rows_high = sem("rows_high")
        rows_loaded = sem("rows_loaded")
        wide_filled = [sem("wide_filled0"), sem("wide_filled1")]
        wide_free = [sem("wide_free0"), sem("wide_free1")]
        narrow_filled = sem("narrow_filled")
        narrow_free = sem("narrow_free")
        probs_ready = sem("probs_ready")
        gate_shifted = sem("gate_shifted")
        gate_exped = sem("gate_exped")
        split_high = sem("split_high")
        res_ready = sem("res_ready")

        z_filled = sem("z_filled")
        z1_ready = sem("z1_ready")
        h0_ready = sem("h0_ready")
        h1_ready = sem("h1_ready")
        hsum_ready = sem("hsum_ready")
        hsum_used = sem("hsum_used")
        out_ready = sem("out_ready")
        out_stored = sem("out_stored")

        block = ctx.enter_context(nc.Block())

        def rounds(eng, attention, unit, after):
            first = Round(eng, 0)
            for _, step, a in PLAN:
                attention(first, step, a)
            for m in range(LAG):
                unit(first, m)

            def slots(this, following):
                at = 0
                for k in range(UNITS):
                    while following and at < len(PLAN) and PLAN[at][0] == k:
                        attention(following, PLAN[at][1], PLAN[at][2])
                        at += 1
                    if k + LAG < UNITS:
                        unit(this, k + LAG)
                    elif following:
                        unit(following, k + LAG - UNITS)
                    after(this, k)
                assert not following or at == len(PLAN)

            with eng.Fori(0, BATCHES - 1) as f:
                slots(Round(eng, f), Round(eng, f + 1))
            slots(Round(eng, BATCHES - 1), None)

        def wide_at(r, step, a):
            n = WIDE[step, a]
            return n % 2, r.at(WPB, n // 2), r.at(WPB, n // 2 + 1)

        def taken(r, step, a):
            n = WIDE[step, a]
            return wide_free[n % 2], r.at(WPB, n // 2 + 1)

        @block.sync
        def _(sp):
            for a in range(2):
                for e in range(4):
                    sp.dma_start(z[:, a, e * DFF:(e + 1) * DFF], W1[4 * a + e]).then_inc(w1_loaded, 16)
            n = 0
            for dst, src in ((t_stage.rearrange("p (m h) -> p m h", h=HEADS),
                              bass.AP(time_bias.tensor, time_bias.offset, [[HEADS, TPT], [HEADS, TIMES], [1, HEADS]])),
                             (p_stage.rearrange("p (m h) -> p m h", h=HEADS),
                              bass.AP(part_bias.tensor, part_bias.offset, [[HEADS, PARTS], [HEADS, PARTS], [1, HEADS]])),
                             (b2_stage, b2), (b1_stage, b1.rearrange("e (t p) -> (e t) p", p=P)),
                             (wqkv[:, 0, :], Wq), (wqkv[:, 1, :], Wk), (wqkv[:, 2, :], Wv), (wg[:, :], Wg),
                             (w2[:, :, :], W2.rearrange("e (t p) d -> p (e t) d", p=P))):
                sp.dma_start(dst, src).then_inc(weights_loaded, 16)
                n += 1
            sp.wait_ge(pool_set, 1)
            for h in range(HEADS):
                c = h % GH
                sp.dma_start(wo_pad[32 * c:32 * c + HD, h // GH, :], Wo[h * HD:(h + 1) * HD, :]).then_inc(weights_loaded, 16)
                n += 1
            assert n == WEIGHT_DMAS

            def load_x(r):
                if not (isinstance(r.b, int) and r.b == 0):
                    sp.wait_ge(res_ready, r.at(CHUNKS, 0))
                for tl in range(TPT):
                    sp.dma_start(xs[tl * PARTS:(tl + 1) * PARTS, :, :],
                                 x[r.b].rearrange("n (i t) c -> t n i c", t=TPT)[tl]).then_inc(x_loaded, 16)

            def attention(r, step, a):
                if step == "norm" and a == 0:
                    load_x(r)
                elif step == "stack":
                    g, hh = a
                    h = g * GH + hh
                    if g == 0:
                        if hh == 0:
                            sp.wait_ge(*taken(r, "key", 0))
                    else:
                        n = WIDE["scores", (0, hh, 2)]
                        sp.wait_ge(wide_filled[n % 2], r.at(WPB, n // 2 + 1))
                    rows = slice(h * HD, (h + 1) * HD)
                    for n, (q, k) in enumerate(((0, 2), (1, 2), (0, 3), (1, 3))):
                        dst = slice(n * HD, (n + 1) * HD)
                        sp.dma_start(qst[dst, hh, :].bitcast(F32), halves[rows, q, :]).then_inc(stack_loaded[hh], 16)
                        sp.dma_start(kst[dst, hh, :].bitcast(F32), halves[rows, k, :]).then_inc(stack_loaded[hh], 16)
                elif step == "rows":
                    sp.wait_ge(*taken(r, "rows", a))
                    for s in range(2):
                        sp.dma_start(qst[64 + s:65 + s, :, :].bitcast(F32).rearrange("p g (i t) -> p (g i) t", t=P),
                                     max_rows[:, s, :]).then_inc(rows_loaded, 16)

            def after(r, k):
                if k % UNITS_PER_CHUNK == UNITS_PER_CHUNK - 1:
                    c = k // UNITS_PER_CHUNK
                    sp.wait_ge(out_ready, r.at(CHUNKS, c + 1 + 1))
                    for tl in range(TPT):
                        dst = out[r.b].rearrange("n (i t) c -> t n i c", t=TPT)[tl]
                        sp.dma_start(dst[:, c * HT:(c + 1) * HT, :],
                                     outt[tl * PARTS:(tl + 1) * PARTS, :, :]).then_inc(out_stored, 16)

            sp.sem_inc(out_stored, 16)
            rounds(sp, attention, lambda r, m: None, after)
            sp.wait_ge(out_stored, 16 * (TPT * CHUNKS * BATCHES + 1))

        @block.gpsimd
        def _(pool):
            for n, (buf, value) in enumerate(((wo_pad[:, :, :], 0.0), (ident[:, :], 0.0), (spread[:, :], 0.0),
                                              (z[0:48, 2, 0:256], 0.0), (rel, 0.0), (val[:, :, :, HD:2 * HD], 1.0),
                                              (kst[64:66, :, :].bitcast(F32), 1.0), (twos, 2.0))):
                if n:
                    pool.wait_ge(pool_set, n)
                pool.memset(buf, value).then_inc(pool_set, 1)
            pool.wait_ge(pool_set, 8)
            pool.affine_select(out=ident[:, :], in_=ident[:, :], compare_op=ALU.not_equal, fill=1.0, base=0,
                               pattern=[[-1, P]], channel_multiplier=1).then_inc(pool_set, 1)
            pool.wait_ge(pool_set, 9)
            pool.affine_select(out=spread[:, :], in_=spread[:, :], compare_op=ALU.not_equal, fill=1.0, base=-HD,
                               pattern=[[-32, GH], [0, 32]], channel_multiplier=1).then_inc(pool_set, 1)
            pool.wait_ge(pool_set, 10)
            done = 10
            for rows, n, pattern in ((slice(0, TPT), TPT, [[-1, TPT], [0, PARTS]]),
                                     (slice(32, 32 + PARTS), PARTS, [[0, TPT], [-1, PARTS]])):
                v = z[rows, 2, 0:128].rearrange("p (a b) -> p a b", a=TPT)
                pool.affine_select(out=v, in_=v, compare_op=ALU.not_equal, fill=1.0, base=0,
                                   pattern=pattern, channel_multiplier=1).then_inc(pool_set, 1)
                done += 1
                pool.wait_ge(pool_set, done)
                v = z[rows, 2, 128:256].rearrange("p (a b) -> p a b", a=TPT)
                pool.affine_select(out=v, in_=v, compare_op=ALU.not_equal, fill=1.0, base=1 - n,
                                   pattern=[[-s, m] for s, m in pattern], channel_multiplier=1).then_inc(pool_set, 1)
                done += 1
                pool.wait_ge(pool_set, done)
            pool.wait_ge(table_used, 4 * HEADS)
            v = key_table[:, :, 0:P].rearrange("p h (t n) -> p h t n", t=TPT)
            pool.affine_select(out=v, in_=v, compare_op=ALU.is_ge, fill=NEG, base=PARTS - 1,
                               pattern=[[0, HEADS], [PARTS, TPT], [0, PARTS]], channel_multiplier=-1).then_inc(setup_done, 1)
            pool.wait_ge(setup_done, 1)
            v = query_table[:, :, TOK - P:TOK].rearrange("p h (t n) -> p h t n", t=TPT)
            pool.affine_select(out=v, in_=v, compare_op=ALU.is_ge, fill=NEG, base=0,
                               pattern=[[0, HEADS], [-PARTS, TPT], [0, PARTS]], channel_multiplier=1).then_inc(setup_done, 1)
            pool.sem_inc(hsum_ready, 2)
            chain = [0]

            def attention(r, step, a):
                if step == "norm":
                    links = 4 * NEWTON - 1
                    pool.wait_ge(ln_seeded, r.at(2, a + 1))
                    chain[0] = links * a

                    def link(ins):
                        chain[0] += 1
                        ins.then_inc(pool_chain, 1)
                        pool.wait_ge(pool_chain, r.at(2 * links, chain[0]))

                    for n in range(NEWTON):
                        link(pool.tensor_tensor(ln_t[:, :], ln_y[:, :], ln_y[:, :], ALU.mult))
                        link(pool.tensor_tensor(ln_t[:, :], ln_t[:, :], ln_v[:, :], ALU.mult))
                        pool.sem_inc(pool_met, 1)
                        link(pool.tensor_scalar(ln_t[:, :], ln_t[:, :], -0.5, 1.5, ALU.mult, ALU.add))
                        if n < NEWTON - 1:
                            link(pool.tensor_tensor(ln_y[:, :], ln_y[:, :], ln_t[:, :], ALU.mult))
                        else:
                            pool.tensor_tensor(ln_y[:, :], ln_y[:, :], ln_t[:, :], ALU.mult).then_inc(ln_rooted, 1)

            def unit(r, m):
                pool.wait_ge(h1_ready, r.at(UNITS, m + 1))
                pool.wait_ge(hsum_used, r.at(UNITS, m + 1))
                pool.tensor_tensor(hsum[:, m % NHS, :], h0[:, m % 2, :], h1[:, m % 2, :],
                                   ALU.add).then_inc(hsum_ready, 1)

            rounds(pool, attention, unit, lambda r, k: None)

        @block.scalar
        def _(act):
            act.wait_ge(setup_filled, 1)
            act.copy(b1_col[:, :], narrow[:, 0:EXPERTS * FT]).then_inc(act_set, 1)
            act.wait_ge(setup_filled, 2)
            act.copy(b2_row[:, :], acc[:, 0:C]).then_inc(act_set, 1)
            act.sem_inc(h0_ready, 2)

            def attention(r, step, a):
                if step in WIDE_STEPS:
                    s, _, filled = wide_at(r, step, a)
                    w = wide[s]
                if step == "turn":
                    act.wait_ge(wide_filled[s], filled)
                    act.copy(act_t[:, :], w[:, 0:TOK]).then_inc(wide_free[s], 1)
                elif step in ("query", "key"):
                    n, scale = (0, HD ** -0.5) if step == "query" else (2, 1.0)
                    act.wait_ge(wide_filled[s], filled)
                    act.activation(halves[:, n, :].bitcast(F32R), w[:, 0:TOK], ACT.Copy, scale=scale).then_inc(high_ready, 1)
                elif step == "value":
                    act.wait_ge(wide_filled[s], filled)
                    act.copy(val[:, :, :, 0:HD], w[:, 0:TOK].rearrange("p (i h d) -> p i h d", h=HEADS, d=HD)
                             ).then_inc(wide_free[s], 1)
                elif step == "rows":
                    act.wait_ge(wide_filled[s], filled)
                    act.activation(max_rows[:, 0, :].bitcast(F32R), w[0:GH * TILES, 0:P], ACT.Copy,
                                   scale=-1.0).then_inc(rows_high, 1)
                elif step == "exp":
                    for hh in range(GH):
                        act.wait_ge(*taken(r, "scores", (a, hh, 2)))
                        act.activation(z[:, hh, :], z[:, hh, :], ACT.Exp).then_inc(probs_ready, 1)
                elif step == "mix":
                    g, qc = a
                    n = NARROW[step, a]
                    cols = QCOLS if qc == 0 else TOK - QCOLS
                    act.wait_ge(narrow_filled, r.at(NPB, n + 1))
                    if g == 0 and qc == 0:
                        for hh in range(GH):
                            act.wait_ge(stack_loaded[hh], r.at(2 * 8 * 16, 2 * 8 * 16))
                    elif g == 1:
                        act.wait_ge(*taken(r, "divide", (0, qc)))
                    act.copy(mixed[:, qc * QCOLS:qc * QCOLS + cols], narrow[:, 0:cols]).then_inc(narrow_free, 1)
                elif step == "gate":
                    act.wait_ge(gate_shifted, r.at(1, 1))
                    act.activation(gate_e[:, :, :], shifted[:, :, :], ACT.Exp).then_inc(gate_exped, 1)
                elif step == "split":
                    act.wait_ge(wide_filled[s], filled)
                    if not (isinstance(r.b, int) and r.b == 0):
                        act.wait_ge(z_filled, r.at(UNITS, (a + 1) * UNITS_PER_CHUNK - UNITS))
                        act.wait_ge(z1_ready, r.at(UNITS, (a + 1) * UNITS_PER_CHUNK - UNITS + 2))
                    act.copy(x0_hi[:, a * CT:(a + 1) * CT], w[:, 0:CT]).then_inc(split_high, 1)
                    act.copy(ratio_b[:, a * CT:(a + 1) * CT], w[:, 512:512 + CT]).then_inc(split_high, 1)

            def unit(r, m):
                j = m % UNITS_PER_CHUNK
                act.wait_ge(hsum_ready, r.at(UNITS, m + 1))
                act.wait_ge(z1_ready, r.at(UNITS, m + 1 + 2))
                act.activation(h0[:, m % 2, :], zps[m % 2][:, 0:CT], ACT.Gelu, bias=b1_col[:, j:j + 1]).then_inc(h0_ready, 1)
                act.activation(h1[:, m % 2, :], h1[:, m % 2, :], ACT.Gelu, bias=b1_col[:, j:j + 1]).then_inc(h1_ready, 1)

            act.wait_ge(act_set, 2)
            rounds(act, attention, unit, lambda r, k: None)

        @block.vector
        def _(vec):
            vec.wait_ge(weights_loaded, 16 * WEIGHT_DMAS)
            vec.wait_ge(pool_set, 14)
            for h in range(HEADS):
                if h >= 1:
                    vec.wait_ge(table_filled, 2 * h)
                vec.tensor_copy(rel[0:TPT, :].rearrange("p (t n) -> p t n", n=PARTS),
                                window(t_stage, h, [[HEADS, TIMES], [0, PARTS]]))
                vec.tensor_copy(rel[32:48, :].rearrange("p (t n) -> p t n", n=PARTS),
                                window(p_stage, h, [[0, TIMES], [HEADS, PARTS]])).then_inc(rel_ready, 1)
                vec.wait_ge(table_filled, 2 * h + 1)
                vec.tensor_copy(key_table[:, h, 512:TOK], wide[0][:, 0:256][:, ::-1]).then_inc(table_used, 1)
                vec.tensor_copy(key_table[:, h, 0:512], wide[0][:, 256:TOK][:, ::-1]).then_inc(table_used, 1)
                vec.wait_ge(table_filled, 2 * h + 2)
                vec.tensor_copy(query_table[:, h, 0:512], wide[1][:, 0:512]).then_inc(table_used, 1)
                vec.tensor_copy(query_table[:, h, 512:TOK], wide[1][:, 512:TOK]).then_inc(table_used, 1)
            vec.wait_ge(w1_loaded, 16 * 8)
            for a in range(2):
                src = z[:, a, 0:2048].rearrange("p (e f) -> p e f", f=DFF)
                vec.tensor_copy(w1_hi[:, 4 * a:4 * a + 4, :], src).then_inc(vec_set, 1)
                vec.wait_ge(vec_set, 2 * a + 1)
                vec.tensor_tensor(w1_lo[:, 4 * a:4 * a + 4, :], src, w1_hi[:, 4 * a:4 * a + 4, :],
                                  ALU.subtract).then_inc(vec_set, 1)
            vec.wait_ge(vec_set, 4)
            vec.wait_ge(setup_done, 2)
            vec.sem_inc(z1_ready, 2)
            vec.sem_inc(out_ready, 1)

            chain = [0]

            def attention(r, step, a):
                def link(ins):
                    chain[0] += 1
                    ins.then_inc(vec_chain, 1)
                    return r.at(VCHAIN, chain[0])

                if step in WIDE_STEPS:
                    s, _, filled = wide_at(r, step, a)
                    w = wide[s]
                if step == "norm":
                    if a == 0:
                        chain[0] = 0
                        vec.wait_ge(x_loaded, r.at(16 * TPT, 16 * TPT))
                    else:
                        vec.wait_ge(*taken(r, "project", 0))
                    for i in range(TILES):
                        ins = vec.bn_stats(stats[:, i, :], xs[:, i, :])
                    done = link(ins)
                    vec.wait_ge(vec_chain, done)
                    vec.sem_inc(vec_met, 1)
                    for i in range(TILES):
                        ins = vec.bn_aggr(moments[:, i, :], stats[:, i, :])
                    vec.wait_ge(vec_chain, link(ins))
                    vec.wait_ge(vec_chain, link(vec.tensor_scalar(ln_v[:, :], moments[:, :, 1], LN_EPS[a], None, ALU.add)))
                    vec.wait_ge(vec_chain, link(vec.tensor_scalar(ln_i[:, :], ln_v[:, :].bitcast(I32), 1, None,
                                                                  ALU.logical_shift_right)))
                    vec.tensor_scalar(ln_y[:, :].bitcast(I32), ln_i[:, :], -1.0, RSQRT_SEED, ALU.mult,
                                      ALU.add).then_inc(ln_seeded, 1)
                    vec.wait_ge(ln_rooted, r.at(2, a + 1))
                    if a == 0 and not (isinstance(r.b, int) and r.b == 0):
                        n = WIDE["split", 1]
                        vec.wait_ge(wide_filled[n % 2], r.at(WPB, n // 2 + 1 - WPB))
                    for i in range(TILES):
                        ins = vec.tensor_scalar(xn[:, i, :], xs[:, i, :], moments[:, i, 0:1], ln_y[:, i:i + 1],
                                                ALU.subtract, ALU.mult)
                    ins.then_inc(xn_ready, 1)
                elif step in ("query", "key"):
                    n, scale = (0, HD ** -0.5) if step == "query" else (2, 1.0)
                    vec.wait_ge(high_ready, r.at(2, 1 + n // 2))
                    vec.scalar_tensor_tensor(out=halves[:, n + 1, :].bitcast(F32R), in0=w[:, 0:TOK], scalar=scale,
                                             in1=halves[:, n, :], op0=ALU.mult, op1=ALU.subtract).then_inc(wide_free[s], 1)
                elif step == "maxima":
                    g, hh, part = a
                    h = g * GH + hh
                    vec.wait_ge(wide_filled[s], filled)
                    vec.sem_inc(vec_met, 1)
                    for i, at in (((5, 0), (1, 768)), ((4, 0), (2, 640)), ((3, 0), (0, 512)))[part]:
                        n = (i + 1) * P
                        ins = vec.tensor_tensor_reduce(w[:, at:at + n], w[:, at:at + n],
                                                       query_table[:, h, TOK - n:TOK], 1.0, -3e38, ALU.add, ALU.max,
                                                       maxes[:, hh * TILES + i:hh * TILES + i + 1])
                    ins.then_inc(wide_free[s], 1)
                elif step == "rows":
                    vec.wait_ge(rows_high, r.at(GROUPS, a + 1))
                    vec.scalar_tensor_tensor(out=max_rows[:, 1, :].bitcast(F32R), in0=w[0:GH * TILES, 0:P], scalar=-1.0,
                                             in1=max_rows[:, 0, :], op0=ALU.mult, op1=ALU.subtract).then_inc(wide_free[s], 1)
                elif step == "scores":
                    g, hh, part = a
                    h = g * GH + hh
                    vec.wait_ge(wide_filled[s], filled)
                    if not (g == 0 and isinstance(r.b, int) and r.b == 0) and hh == 0 and part == 0:
                        n = NARROW["mix", (1 - g, 1)]
                        vec.wait_ge(narrow_filled, r.at(NPB, n + 1 - (NPB if g == 0 else 0)))
                    zh, kt = z[:, hh, :], key_table[:, h, :]
                    if part == 0:
                        vec.tensor_tensor(zh[:, 0:512], w[:, 0:512], kt[:, 0:512], ALU.add)
                        ins = vec.tensor_tensor(zh[:, 512:896], w[:, 512:896], kt[:, 0:384], ALU.add)
                    elif part == 1:
                        vec.tensor_tensor(window(zh, 896, [[256, 2], [1, 256]]), window(w[:, :], 0, [[256, 2], [1, 256]]),
                                          window(kt, 0, [[0, 2], [1, 256]]), ALU.add)
                        ins = vec.tensor_tensor(window(zh, 1408, [[128, 2], [1, 128]]),
                                                window(w[:, :], 512, [[128, 2], [1, 128]]),
                                                window(kt, 0, [[0, 2], [1, 128]]), ALU.add)
                    else:
                        ins = vec.tensor_tensor(window(zh, 1664, [[256, 4], [1, 256]]),
                                                window(w[:, :], 0, [[256, 4], [1, 256]]),
                                                window(kt, 128, [[128, 4], [1, 256]]), ALU.add)
                    ins.then_inc(wide_free[s], 1)
                elif step == "divide":
                    g, qc = a
                    cols = QCOLS if qc == 0 else TOK - QCOLS
                    vec.wait_ge(wide_filled[s], filled)
                    if (g, qc) != (0, 0):
                        vec.wait_ge(*taken(r, "divide", ((2 * g + qc - 1) // 2, 1 - qc)))
                    done = link(vec.reciprocal(recip[:, 0:cols], w[:, 0:cols]))
                    vec.wait_ge(vec_chain, done)
                    q0 = qc * QCOLS
                    vec.tensor_tensor(mixed_n[:, g, q0:q0 + cols], mixed[:, q0:q0 + cols], recip[:, 0:cols],
                                      ALU.mult).then_inc(wide_free[s], 1)
                elif step == "project":
                    vec.wait_ge(wide_filled[s], filled)
                    vec.tensor_tensor(xs[:, :, :], w[:, 0:TOK].rearrange("p (i c) -> p i c", c=C),
                                      xs[:, :, :], ALU.add).then_inc(wide_free[s], 1)
                elif step == "gate":
                    n = NARROW[step, a]
                    vec.wait_ge(narrow_filled, r.at(NPB, n + 1))
                    vec.sem_inc(vec_met, 1)
                    for i in range(TILES):
                        ins = vec.max(sorted_l[:, i, :], narrow[:, i * EXPERTS:(i + 1) * EXPERTS])
                    ins.then_inc(narrow_free, 1)
                    vec.wait_ge(narrow_free, r.at(NPB, n + 1))
                    vec.tensor_tensor(shifted[:, :, :], sorted_l[:, :, :], window(sorted_l[:, 0, :], 0, [[EXPERTS, TILES], [0, EXPERTS]]),
                                      ALU.subtract).then_inc(gate_shifted, 1)
                    vec.wait_ge(gate_exped, r.at(1, 1))
                    vec.wait_ge(vec_chain, link(vec.tensor_reduce(gate_s[:, :, 0], gate_e[:, :, :], AX.X, ALU.add)))
                    vec.wait_ge(vec_chain, link(vec.reciprocal(gate_s[:, :, 1], gate_s[:, :, 0])))
                    vec.wait_ge(vec_chain, link(vec.tensor_tensor(probs[:, :, :], gate_e[:, :, 0:2],
                                                                  window(gate_s[:, 0, :], 1, [[4, TILES], [0, 2]]), ALU.mult)))
                    vec.wait_ge(vec_chain, link(vec.tensor_reduce(gate_s[:, :, 2], probs[:, :, :], AX.X, ALU.add)))
                    vec.wait_ge(vec_chain, link(vec.reciprocal(gate_s[:, :, 3], gate_s[:, :, 2])))
                    vec.wait_ge(vec_chain, link(vec.tensor_tensor(top[:, :, :], probs[:, :, :],
                                                                  window(gate_s[:, 0, :], 3, [[4, TILES], [0, 2]]), ALU.mult)))
                    vec.wait_ge(vec_chain, link(vec.reciprocal(ratio[:, :, 0], top[:, :, 0])))
                    vec.tensor_tensor(ratio[:, :, 1], top[:, :, 1], ratio[:, :, 0], ALU.mult)
                    for i in range(TILES):
                        ins = vec.tensor_scalar(xn[:, i, :], xn[:, i, :], top[:, i, 0:1], None, ALU.mult)
                    ins.then_inc(xn_ready, 1)
                    assert chain[0] == VCHAIN
                elif step == "split":
                    vec.wait_ge(split_high, r.at(4, 2 * a + 2))
                    ins = vec.tensor_tensor(x0_lo[:, a * CT:(a + 1) * CT], w[:, 0:CT], x0_hi[:, a * CT:(a + 1) * CT],
                                            ALU.subtract)
                    ins.then_inc(wide_free[s], 1)
                    if not (isinstance(r.b, int) and r.b == 0) and a == 0:
                        vec.wait_ge(out_ready, r.at(CHUNKS, 1 - CHUNKS + 1))
                    if a == 0:
                        residual(r, 0)
                    elif isinstance(r.b, int) and r.b == 0:
                        residual(r, 1)

            def residual(r, c):
                ts = slice(c * HT, (c + 1) * HT)
                vec.tensor_tensor(res[:, ts, :], xs[:, ts, :], window(b2_row[:, :], 0, [[0, HT], [1, C]]),
                                  ALU.add).then_inc(res_ready, 1)

            def unit(r, m):
                c = m // UNITS_PER_CHUNK
                vec.wait_ge(z_filled, r.at(UNITS, m + 1))
                vec.wait_ge(hsum_ready, r.at(UNITS, m + 1))
                vec.tensor_tensor(h1[:, m % 2, :], zps[m % 2][:, 0:CT], ratio_b[:, c * CT:(c + 1) * CT],
                                  ALU.mult).then_inc(z1_ready, 1)

            def after(r, k):
                if k % UNITS_PER_CHUNK == UNITS_PER_CHUNK - 1:
                    c = k // UNITS_PER_CHUNK
                    vec.wait_ge(hsum_used, r.at(UNITS, k + 1 + NHS))
                    vec.wait_ge(out_stored, r.at(16 * TPT * CHUNKS, 16 * (TPT * c + 1)))
                    vec.wait_ge(res_ready, r.at(CHUNKS, c + 1))
                    vec.tensor_tensor(outt[:, :, :], acc[:, 0:CT].rearrange("p (i c) -> p i c", c=C),
                                      res[:, c * HT:(c + 1) * HT, :], ALU.add).then_inc(out_ready, 1)
                    if c == 1 and not isinstance(r.b, int):
                        vec.wait_ge(out_ready, r.at(CHUNKS, CHUNKS + 1))
                        residual(r, 1)

            rounds(vec, attention, unit, after)

        @block.tensor
        def _(pe):
            pe.wait_ge(pool_set, 14)
            pe.wait_ge(weights_loaded, 16 * WEIGHT_DMAS)
            pe.transpose(narrow[:, 0:EXPERTS * FT], b1_stage, ident[0:32, 0:32]).then_inc(setup_filled, 1)
            pe.matmul(acc[:, 0:C], twos, b2_stage, start=True, stop=True).then_inc(setup_filled, 1)
            for h in range(HEADS):
                pe.wait_ge(rel_ready, h + 1)
                if h >= 1:
                    pe.wait_ge(table_used, 4 * h)
                for n in range(2):
                    pe.matmul(wide[n][:, 0:512], one_hot[n], rel[:, 0:512], start=True, stop=True)
                    pe.matmul(wide[n][:, 512:TOK], one_hot[n], rel[:, 512:TOK], start=True,
                              stop=True).then_inc(table_filled, 1)
            pe.wait_ge(act_set, 2)
            pe.wait_ge(table_used, 4 * HEADS)
            pe.wait_ge(vec_set, 4)
            pe.wait_ge(setup_done, 2)
            pe.sem_inc(hsum_used, NHS)

            def attention(r, step, a):
                if step in WIDE_STEPS:
                    s, free, _ = wide_at(r, step, a)
                    w = wide[s]
                    if not (isinstance(free, int) and free <= 0):
                        pe.wait_ge(wide_free[s], free)
                if step in NARROW_STEPS:
                    free = r.at(NPB, NARROW[step, a])
                    if not (isinstance(free, int) and free <= 0):
                        pe.wait_ge(narrow_free, free)
                if step == "turn":
                    pe.wait_ge(xn_ready, r.at(3, a + 1))
                    for i in range(TILES):
                        ins = pe.transpose(w[:, i * P:(i + 1) * P], xn[:, i, :], ident[:, :])
                    ins.then_inc(wide_filled[s], 1)
                elif step in ("query", "key"):
                    pe.wait_ge(*taken(r, "turn", 0))
                    n = 0 if step == "query" else 1
                    pe.matmul(w[:, 0:512], wqkv[:, n, :], act_t[:, 0:512], start=True, stop=True)
                    pe.matmul(w[:, 512:TOK], wqkv[:, n, :], act_t[:, 512:TOK], start=True,
                              stop=True).then_inc(wide_filled[s], 1)
                elif step == "value":
                    for i in range(TILES):
                        ins = pe.matmul(w[:, i * P:(i + 1) * P], act_t[:, i * P:(i + 1) * P], wqkv[:, 2, :],
                                        start=True, stop=True)
                    ins.then_inc(wide_filled[s], 1)
                elif step == "maxima":
                    g, hh, part = a
                    if part == 0:
                        pe.wait_ge(stack_loaded[hh], r.at(2 * 8 * 16, (g + 1) * 8 * 16))
                    for i, k0, k1, at in (((5, 0, 512, 0), (5, 512, 768, 512), (1, 0, 256, 768)),
                                          ((4, 0, 512, 0), (4, 512, 640, 512), (2, 0, 384, 640)),
                                          ((3, 0, 512, 0), (0, 0, 128, 512)))[part]:
                        ins = pe.matmul(w[:, at:at + k1 - k0], qst[0:64, hh, i * P:(i + 1) * P],
                                        kst[0:64, hh, k0:k1], start=True, stop=True)
                    ins.then_inc(wide_filled[s], 1)
                elif step == "rows":
                    pe.wait_ge(*taken(r, "maxima", (a, GH - 1, 2)))
                    pe.transpose(w[0:GH * TILES, 0:P], maxes[:, :], ident[:, :]).then_inc(wide_filled[s], 1)
                elif step == "scores":
                    g, hh, part = a
                    if hh == 0 and part == 0:
                        pe.wait_ge(rows_loaded, r.at(2 * 16 * GROUPS, 2 * 16 * (g + 1)))
                    for i, q0, q1, at in (((0, 0, 512, 0), (1, 128, 512, 512)),
                                          ((2, 256, 512, 0), (4, 512, 768, 256), (3, 384, 512, 512), (5, 640, 768, 640)),
                                          ((3, 512, 768, 0), (2, 512, 768, 256), (1, 512, 768, 512), (0, 512, 768, 768)))[part]:
                        ins = pe.matmul(w[:, at:at + q1 - q0], kst[:, hh, i * P:(i + 1) * P],
                                        qst[:, hh, q0:q1], start=True, stop=True)
                    ins.then_inc(wide_filled[s], 1)
                elif step == "mix":
                    g, qc = a
                    tiles = ((0, 0), (1, 128), (2, 256), (3, 384)) if qc == 0 else \
                        ((0, 0), (1, 0), (2, 0), (3, 0), (4, 0), (5, 128))
                    width = QCOLS if qc == 0 else TOK - QCOLS
                    for n, (i, q0) in enumerate(tiles):
                        for hh in range(GH):
                            if n == 0:
                                if qc == 0:
                                    pe.wait_ge(probs_ready, r.at(HEADS, g * GH + hh + 1))
                            at = Z_AT[i, qc]
                            ins = pe.matmul(narrow[32 * hh:32 * hh + 32, q0:width], val[:, i, g * GH + hh, :],
                                            z[:, hh, at:at + width - q0], start=(n == 0), stop=(n == len(tiles) - 1))
                    ins.then_inc(narrow_filled, 1)
                elif step == "divide":
                    g, qc = a
                    cols = QCOLS if qc == 0 else TOK - QCOLS
                    pe.wait_ge(narrow_free, r.at(NPB, NARROW["mix", a] + 1))
                    pe.matmul(w[:, 0:cols], spread[:, :], mixed[:, qc * QCOLS:qc * QCOLS + cols], start=True,
                              stop=True).then_inc(wide_filled[s], 1)
                elif step == "project":
                    for qc in range(2):
                        pe.wait_ge(*taken(r, "divide", (1, qc)))
                    for i in range(TILES):
                        for g in range(GROUPS):
                            ins = pe.matmul(w[:, i * P:(i + 1) * P], mixed_n[:, g, i * P:(i + 1) * P], wo_pad[:, g, :],
                                            start=(g == 0), stop=(g == GROUPS - 1))
                    ins.then_inc(wide_filled[s], 1)
                elif step == "gate":
                    pe.wait_ge(*taken(r, "turn", 1))
                    for i in range(TILES):
                        ins = pe.matmul(narrow[:, i * EXPERTS:(i + 1) * EXPERTS], act_t[:, i * P:(i + 1) * P], wg[:, :],
                                        start=True, stop=True)
                    ins.then_inc(narrow_filled, 1)
                elif step == "split":
                    pe.wait_ge(xn_ready, r.at(3, 3))
                    for n in range(HT):
                        i = a * HT + n
                        pe.transpose(w[:, n * P:(n + 1) * P], xn[:, i, :], ident[:, :])
                        ins = pe.transpose(w[:, 512 + n * P:512 + (n + 1) * P],
                                           ratio[:, i, 1:2].broadcast_to([P, P]), ident[:, :])
                    ins.then_inc(wide_filled[s], 1)

            def unit(r, m):
                c, j = divmod(m, UNITS_PER_CHUNK)
                e, t = divmod(j, FT)
                if j == 0:
                    pe.wait_ge(*taken(r, "split", c))
                pe.wait_ge(h0_ready, r.at(UNITS, m + 1))
                cols = slice(c * CT, (c + 1) * CT)
                zp = zps[m % 2][:, 0:CT]
                hi, lo = w1_hi[:, e, t * P:(t + 1) * P], w1_lo[:, e, t * P:(t + 1) * P]
                pe.matmul(zp, lo, x0_hi[:, cols], start=True, stop=False)
                pe.matmul(zp, hi, x0_lo[:, cols], start=False, stop=False)
                pe.matmul(zp, hi, x0_hi[:, cols], start=False, stop=True).then_inc(z_filled, 1)

            def after(r, k):
                c, j = divmod(k, UNITS_PER_CHUNK)
                pe.wait_ge(hsum_ready, r.at(UNITS, k + 1 + 2))
                if j == 0:
                    pe.wait_ge(out_ready, r.at(CHUNKS, c + 1))
                for n in range(HT):
                    ins = pe.matmul(acc[:, n * P:(n + 1) * P], hsum[:, k % NHS, n * P:(n + 1) * P], w2[:, j, :],
                                    start=(j == 0 and n == 0), stop=(j == UNITS_PER_CHUNK - 1), skip_group_check=True)
                ins.then_inc(hsum_used, 1)

            rounds(pe, attention, unit, after)


WEIGHT_DMAS = 9 + HEADS
_INS = ["x", "L0_conv_Wq", "L0_conv_Wk", "L0_conv_Wv", "L0_conv_Wo", "L0_conv_rel_pos_bias",
        "L0_conv_particle_rel_pos_bias", "L0_ffn_Wg", "L0_ffn_W1", "L0_ffn_b1", "L0_ffn_W2", "L0_ffn_b2"]


def kernel(**inputs):
    import numpy as np
    import concourse.bacc as bacc
    from concourse.bass_utils import run_bass_kernel_spmd

    nc = bacc.Bacc("TRN2", target_bir_lowering=False, num_devices=1)
    arrays, args = {}, []
    for name in _INS:
        a = np.ascontiguousarray(inputs[name])
        arrays[f"in_{name}"] = a
        args.append(nc.dram_tensor(f"in_{name}", a.shape, mybir.dt.from_np(a.dtype), kind="ExternalInput").ap())
    args.append(nc.dram_tensor("out_dram", (BATCHES, PARTS, TIMES, C), F32, kind="ExternalOutput").ap())
    build(nc, *args)
    r = run_bass_kernel_spmd(nc, [arrays], core_ids=[0])
    return r.results[0]["out_dram"]
```

```python
from contextlib import ExitStack

import concourse.bass as bass
from concourse import mybir

F32 = mybir.dt.float32
F32R = mybir.dt.float32r
BF16 = mybir.dt.bfloat16
I32 = mybir.dt.int32
ALU = mybir.AluOpType
ACT = mybir.ActivationFunctionType
AX = mybir.AxisListType

P = 128
BATCHES, PARTS, TIMES, C = 16, 16, 48, 128
HEADS, HD = 8, 16
TOK = PARTS * TIMES
TPT = P // PARTS
TILES = TOK // P
GH = 4
GROUPS = HEADS // GH
EXPERTS, DFF = 8, 512
FT = DFF // P
UNITS_PER_CHUNK = EXPERTS * FT
CHUNKS = 2
CT = TOK // CHUNKS
HT = TILES // CHUNKS
UNITS = CHUNKS * UNITS_PER_CHUNK
LAG = 4
NHS = 4
QCOLS = 512
ZW = 2688
NEG = -1e30
LN_EPS = (1e-6, 1e-5)
RSQRT_SEED = 1597463007.0
NEWTON = 3

Z_AT = {(0, 0): 0, (1, 0): 512, (2, 0): 896, (4, 1): 1152, (3, 0): 1408, (5, 1): 1536,
        (3, 1): 1664, (2, 1): 1920, (1, 1): 2176, (0, 1): 2432}


def attention_plan():
    def maxima(g, slots):
        return [(slot, "maxima", (g, n // 3, n % 3)) for n, slot in enumerate(slots)]

    plan = [(-5, "stats", 0), (-5, "seed", 0), (-4, "root", (0, 0)), (-4, "root", (0, 1)), (-4, "root", (0, 2)),
            (-3, "scale", (0, 0)), (-2, "scale", (0, 1)), (0, "turn", 0), (2, "query", 0), (2, "key", 0), (4, "value", 0)]
    plan += [(4, "stack", (0, hh)) for hh in range(GH)]
    plan += maxima(0, (8, 9, 10, 11, 12, 13, 14, 15, 16, 17, 18, 20)) + [(22, "rows", 0)]
    for hh in range(GH):
        plan += [(26, "scores", (0, hh, n)) for n in range(3)] + [(26, "stack", (1, hh))]
    plan += [(27, "mix", (0, 0)), (28, "mix", (0, 1))]
    late = [(30, "sums", 0), (32, "divide", 0)] + maxima(1, (31, 31, 32, 33, 34, 36, 36, 37, 38, 39, 39, 40))
    plan += sorted(late, key=lambda step: step[0]) + [(41, "rows", 1)]
    plan += [(44, "scores", (1, n // 3, n % 3)) for n in range(12)]
    plan += [(44, "mix", (1, 0)), (45, "mix", (1, 1)), (46, "sums", 1), (47, "divide", 1), (49, "project", 0), (50, "load", 1)]
    plan += [(50, "stats", 1), (51, "seed", 1), (51, "root", (1, 0)), (52, "root", (1, 1)), (52, "root", (1, 2)),
             (54, "scale", (1, 0)), (54, "scale", (1, 1)), (56, "turn", 1), (57, "gate", 0), (58, "weigh", 0),
             (60, "split", 0), (60, "split", 1)]
    return plan


PLAN = attention_plan()
WIDE_STEPS = ("turn", "query", "key", "value", "maxima", "rows", "scores", "sums", "divide", "project", "split")
NARROW_STEPS = ("mix", "gate")
WIDE = {(s, a): n for n, (s, a) in enumerate([(s, a) for _, s, a in PLAN if s in WIDE_STEPS])}
NARROW = {(s, a): n for n, (s, a) in enumerate([(s, a) for _, s, a in PLAN if s in NARROW_STEPS])}
assert len(WIDE) % 2 == 0
WPB = len(WIDE) // 2
NPB = len(NARROW)
VCHAIN = 2 * (5 + 3 * NEWTON) + 7
NH1 = 4


class Round:

    def __init__(self, eng, b):
        self.eng, self.b, self.base = eng, b, {}

    def at(self, per, n):
        if isinstance(self.b, int):
            return per * self.b + n
        if per not in self.base:
            self.base[per] = self.eng.snap(self.b * per)
        return self.base[per] + n


def window(ap, offset, dims):
    return bass.AP(ap.tensor, ap.offset + offset, [list(ap.ap[0])] + [list(d) for d in dims])


def build(nc, x, Wq, Wk, Wv, Wo, time_bias, part_bias, Wg, W1, b1, W2, b2, out):
    with ExitStack() as ctx:
        def sb(name, shape, dt=F32):
            return ctx.enter_context(nc.sbuf_tensor(name, shape, dt))

        def ps(name, shape):
            return ctx.enter_context(nc.psum_tensor(name, shape, F32))

        def sem(name):
            return ctx.enter_context(nc.semaphore(name))

        w1_hi = sb("w1_hi", [P, EXPERTS, DFF], F32R)
        w1_lo = sb("w1_lo", [P, EXPERTS, DFF], F32R)
        w2 = sb("w2", [P, EXPERTS * FT, C])
        b1_col = sb("b1_col", [P, EXPERTS * FT])
        b2_row = sb("b2_row", [P, C])
        wqkv = sb("wqkv", [P, 3, C])
        wo_pad = sb("wo_pad", [P, GROUPS, C])
        wg = sb("wg", [P, EXPERTS])
        ident = sb("ident", [P, P])
        pick = sb("pick", [P, GH])
        bias_rows = sb("bias_rows", [P, GH, TOK], F32R)
        key_hot = sb("key_hot", [P, GROUPS, P], F32R)
        query_table = sb("query_table", [P, HEADS, TOK], BF16)
        x_in = sb("x_in", [P, TILES, C])
        xs = sb("xs", [P, TILES, C])
        xn = sb("xn", [P, TILES, C])
        act_t = sb("act_t", [P, TOK])
        halves = sb("halves", [P, 4, TOK])
        mixed = sb("mixed", [P, TOK])
        mixed_n = [act_t, halves[:, 1, :]]
        val = sb("val", [P, TILES, HEADS, 2 * HD])
        stack = sb("stack", [P, 2, GH, TOK], F32R)
        qst, kst = stack[:, 0], stack[:, 1]
        z = sb("z", [P, GH, ZW])
        maxes = sb("maxes", [P, GH * TILES])
        recip = sb("recip", [P, TILES, GH])
        max_rows = sb("max_rows", [GH * TILES, 2, P])
        stats = act_t[:, 0:TILES * 6].rearrange("p (i s) -> p i s", s=6)
        moments = sb("moments", [P, TILES, 2])
        ln_v = sb("ln_v", [P, TILES])
        ln_i = sb("ln_i", [P, TILES], I32)
        ln_y = sb("ln_y", [P, TILES])
        ln_t = sb("ln_t", [P, TILES])
        sorted_l, shifted, gate_e = (halves[:, 3, QCOLS + 48 * n:QCOLS + 48 * (n + 1)].rearrange(
            "p (i e) -> p i e", e=EXPERTS) for n in range(3))
        gate_s = sb("gate_s", [P, TILES, 4])
        probs = sb("probs", [P, TILES, 2])
        top = sb("top", [P, TILES, 2])
        ratio = sb("ratio", [P, TILES, 2])
        x0_hi = sb("x0_hi", [P, TOK], F32R)
        x0_lo = sb("x0_lo", [P, TOK], F32R)
        ratio_b = sb("ratio_b", [P, TOK])
        res = sb("res", [P, TILES, C])
        h0 = sb("h0", [P, 2, CT])
        h1 = sb("h1", [P, NH1, CT])
        hsum = sb("hsum", [P, NHS, CT])
        outt = sb("outt", [P, HT, C])

        wide = [ps("wide0", [P, 1024]), ps("wide1", [P, 1024])]
        zps = [ps("zps0", [P, 512]), ps("zps1", [P, 512])]
        acc = ps("acc", [P, 512])
        narrow = ps("narrow", [P, 512])

        one_hot = z[0:48, 2, 0:128]
        hot_stage = z[0:48, 2, 128:256]
        z_flat = z[:, :, :].rearrange("p g c -> p (g c)")
        raw = [w2[:, 0:GH * TOK // C, :].rearrange("p e d -> p (e d)").rearrange("p (h t) -> p h t", h=GH), z_flat[:, 6912:6912 + GH * TOK].rearrange("p (h t) -> p h t", h=GH)]
        t_stage = z[0:8, 2, 256:256 + 48 * 8]
        p_stage = z[32:48, 2, 256:256 + 16 * 8]
        b2_stage = z[0:8, 2, 768:896]
        twos = z[0:8, 2, 896:1024]
        b1_stage = z[0:32, 2, 1024:1152]
        rel_stage = z_flat[0:48, 9984:9984 + TOK]
        rel = [rel_stage[:, n * TOK // 2:(n + 1) * TOK // 2].bitcast(BF16) for n in range(2)]
        bias_hi = [w[:, :, :].rearrange("p e f -> p (e f)")[:, 0:GH * TOK].rearrange("p (h t) -> p h t", h=GH)
                   for w in (w1_hi, w1_lo)]
        one_hot16 = z[0:48, 2, 1152:1152 + P // 2].bitcast(BF16)

        biases_loaded = sem("biases_loaded")
        weights_loaded = sem("weights_loaded")
        w1_high = sem("w1_high")
        w1_loaded = sem("w1_loaded")
        w2_loaded = sem("w2_loaded")
        pool_set = sem("pool_set")
        w1_low = sem("w1_low")
        raw_ready = sem("raw_ready")
        raw_masked = sem("raw_masked")
        rel_ready = sem("rel_ready")
        bias_high = sem("bias_high")
        bias_low = [sem("bias_low0"), sem("bias_low1")]
        bias_placed = sem("bias_placed")
        table_filled = sem("table_filled")
        table_used = sem("table_used")
        setup_filled = sem("setup_filled")
        setup_done = sem("setup_done")
        act_set = sem("act_set")

        vec_met = sem("vec_met")
        sp_met = sem("sp_met")
        x_loaded = sem("x_loaded")
        vec_chain = sem("vec_chain")
        xn_ready = sem("xn_ready")
        high_ready = sem("high_ready")
        stack_loaded = [sem(f"stack_loaded{n}") for n in range(GH)]
        rows_high = sem("rows_high")
        rows_loaded = sem("rows_loaded")
        wide_filled = [sem("wide_filled0"), sem("wide_filled1")]
        wide_free = [sem("wide_free0"), sem("wide_free1")]
        narrow_filled = sem("narrow_filled")
        narrow_free = sem("narrow_free")
        gate_shifted = sem("gate_shifted")
        gate_exped = sem("gate_exped")
        split_high = sem("split_high")
        res_ready = sem("res_ready")

        z_filled = sem("z_filled")
        z1_ready = sem("z1_ready")
        h0_ready = sem("h0_ready")
        h1_ready = sem("h1_ready")
        hsum_ready = sem("hsum_ready")
        hsum_used = sem("hsum_used")
        out_ready = sem("out_ready")
        out_stored = sem("out_stored")

        block = ctx.enter_context(nc.Block())

        def rounds(eng, attention, unit, after, last=(), prepare=None):
            first = Round(eng, 0)
            for _, step, a in PLAN:
                attention(first, step, a)
                if prepare:
                    prepare(first, step, a)
            for slot, step, a in PLAN:
                if slot < 0:
                    attention(Round(eng, 1), step, a)
            for m in range(LAG):
                unit(first, m)

            def slots(this, following, ahead):
                def steps(k, late):
                    for r, start in ((following, 0), (ahead, UNITS)):
                        for slot, step, a in PLAN if r else ():
                            if slot + start == k and (step in last) == late:
                                attention(r, step, a)

                for k in range(UNITS):
                    steps(k, False)
                    if k + LAG < UNITS:
                        unit(this, k + LAG)
                    elif following:
                        unit(following, k + LAG - UNITS)
                    after(this, k)
                    steps(k, True)

            with eng.Fori(0, BATCHES - 1) as f:
                slots(Round(eng, f), Round(eng, f + 1), Round(eng, f + 2))
            slots(Round(eng, BATCHES - 1), None, None)

        def lower_biases(eng, g):
            for n, (row, count) in enumerate(((0, TPT), (32, PARTS))):
                eng.wait_ge(bias_high, 2 * g + n + 1)
                if n:
                    eng.wait_ge(bias_low[g], n)
                rows = slice(row, row + count)
                eng.tensor_tensor(raw[g][rows, :, :], raw[g][rows, :, :], bias_hi[g][rows], ALU.subtract).then_inc(bias_low[g], 1)

        def wide_at(r, step, a):
            n = WIDE[step, a]
            return n % 2, r.at(WPB, n // 2), r.at(WPB, n // 2 + 1)

        def taken(r, step, a):
            n = WIDE[step, a]
            return wide_free[n % 2], r.at(WPB, n // 2 + 1)

        @block.sync
        def _(sp):
            def load_x(b):
                for tl in range(TPT):
                    sp.dma_start(x_in[tl * PARTS:(tl + 1) * PARTS, :, :],
                                 x[b].rearrange("n (i t) c -> t n i c", t=TPT)[tl]).then_inc(x_loaded, 16)

            for dst, src in ((t_stage.rearrange("p (m h) -> p m h", h=HEADS),
                              bass.AP(time_bias.tensor, time_bias.offset, [[HEADS, TPT], [HEADS, TIMES], [1, HEADS]])),
                             (p_stage.rearrange("p (m h) -> p m h", h=HEADS),
                              bass.AP(part_bias.tensor, part_bias.offset, [[HEADS, PARTS], [HEADS, PARTS], [1, HEADS]])),
                             (b2_stage, b2), (b1_stage, b1.rearrange("e (t p) -> (e t) p", p=P))):
                sp.dma_start(dst, src).then_inc(biases_loaded, 16)
            load_x(0)
            n = 0
            for dst, src in ((wqkv[:, 0, :], Wq), (wqkv[:, 1, :], Wk), (wqkv[:, 2, :], Wv), (wg[:, :], Wg)):
                sp.dma_start(dst, src).then_inc(weights_loaded, 16)
                n += 1
            sp.wait_ge(pool_set, 1)
            for h in range(HEADS):
                c = h % GH
                sp.dma_start(wo_pad[32 * c:32 * c + HD, h // GH, :], Wo[h * HD:(h + 1) * HD, :]).then_inc(weights_loaded, 16)
                n += 1
            assert n == WEIGHT_DMAS

            def prepare(r, step, a):
                if (step, a) == ("stack", (0, GH - 1)):
                    for g in range(GROUPS):
                        sp.wait_ge(pool_set, POOL_SET)
                        sp.wait_ge(bias_high, 2 * (g + 1))
                        sp.wait_ge(bias_low[g], 2)
                        for row, n, half, src in ((0, TPT, bias_hi[g], 0), (TPT, TPT, raw[g], 0),
                                                  (16, PARTS, bias_hi[g], 32), (32, PARTS, raw[g], 32)):
                            to = slice(64 * g + row, 64 * g + row + n)
                            sp.dma_start(bias_rows[to, :, :].bitcast(F32), (half[src:src + n, :, :] if half is raw[g] else half[src:src + n, :, :].bitcast(F32))).then_inc(bias_placed, 16)
                            sp.dma_start(key_hot[to, g, :].bitcast(F32), hot_stage[src:src + n, :]).then_inc(bias_placed, 16)
                    sp.wait_ge(bias_placed, 16 * BIAS_DMAS)
                    sp.dma_start(w2[:, :, :], W2.rearrange("e (t p) d -> p (e t) d", p=P)).then_inc(w2_loaded, 16)
                elif (step, a) == ("mix", (1, 1)):
                    sp.wait_ge(narrow_filled, NARROW["mix", (1, 1)] + 1)
                    for a in range(2):
                        for e in range(4):
                            sp.dma_start(z[:, a, e * DFF:(e + 1) * DFF], W1[4 * a + e]).then_inc(w1_loaded, 16)

            def attention(r, step, a):
                if step == "load":
                    following = (r.b + 1) % BATCHES if isinstance(r.b, int) else sp.snap((r.b + 1) & (BATCHES - 1))
                    sp.wait_ge(*taken(r, "project", 0))
                    sp.sem_inc(sp_met, 1)
                    load_x(following)
                elif step == "stack":
                    g, hh = a
                    h = g * GH + hh
                    if g == 0:
                        if hh == 0:
                            sp.wait_ge(*taken(r, "key", 0))
                    else:
                        n = WIDE["scores", (0, hh, 2)]
                        sp.wait_ge(wide_filled[n % 2], r.at(WPB, n // 2 + 1))
                    rows = slice(h * HD, (h + 1) * HD)
                    for n, (q, k) in enumerate(((0, 2), (1, 2), (0, 3), (1, 3))):
                        sp.dma_start(stack[n * HD:(n + 1) * HD, :, hh, :].bitcast(F32),
                                     window(halves[rows, q, :], 0, [[(k - q) * TOK, 2], [1, TOK]])).then_inc(stack_loaded[hh], 16)
                elif step == "rows":
                    sp.wait_ge(*taken(r, "rows", a))
                    for s in range(2):
                        sp.dma_start(qst[64 + s:65 + s, :, :].bitcast(F32).rearrange("p g (i t) -> p (g i) t", t=P),
                                     max_rows[:, s, :]).then_inc(rows_loaded, 16)

            def after(r, k):
                if k % UNITS_PER_CHUNK == UNITS_PER_CHUNK - 1:
                    c = k // UNITS_PER_CHUNK
                    sp.wait_ge(out_ready, r.at(CHUNKS, c + 1 + 1))
                    for tl in range(TPT):
                        dst = out[r.b].rearrange("n (i t) c -> t n i c", t=TPT)[tl]
                        sp.dma_start(dst[:, c * HT:(c + 1) * HT, :],
                                     outt[tl * PARTS:(tl + 1) * PARTS, :, :]).then_inc(out_stored, 16)

            sp.sem_inc(out_stored, 16)
            rounds(sp, attention, lambda r, m: None, after, prepare=prepare)
            sp.wait_ge(x_loaded, 16 * TPT * (BATCHES + 1))
            sp.wait_ge(out_stored, 16 * (TPT * CHUNKS * BATCHES + 1))

        @block.gpsimd
        def _(pool):
            cleared = ((wo_pad[:, :, :], 0.0), (ident[:, :], 0.0), (hot_stage, 0.0), (one_hot, 0.0), (pick[:, :], 0.0),
                       (twos, 2.0), (key_hot[:, :, :].bitcast(F32), 0.0), (rel_stage, 0.0), (val[:, :, :, HD:2 * HD], 1.0))
            later = ((bias_rows[:, :, :].bitcast(F32), 0.0), (qst[64:P, :, :].bitcast(F32), 0.0),
                     (kst[64:P, :, :].bitcast(F32), 0.0), (kst[64:66, :, :].bitcast(F32), 1.0))
            done = 0
            for buf, value in cleared:
                if done:
                    pool.wait_ge(pool_set, done)
                pool.memset(buf, value).then_inc(pool_set, 1)
                done += 1
            times, parts = [[1, TPT], [0, PARTS]], [[0, TPT], [1, PARTS]]
            hots = [(ident[:, :], 0, [[-1, P]]), (pick[:, :], -HD, [[-32, GH]])]
            hots += [(one_hot[0:TPT, :], 1 - TPT, times), (one_hot[32:48, :], 1 - PARTS, parts)]
            times, parts = [[-1, TPT], [0, PARTS]], [[0, TPT], [-1, PARTS]]
            hots += [(hot_stage[0:TPT, :], 0, times), (hot_stage[32:48, :], 0, parts)]
            for buf, base, pattern in hots:
                if len(pattern) == 2:
                    buf = buf.rearrange("p (a b) -> p a b", a=pattern[0][1])
                pool.wait_ge(pool_set, done)
                pool.affine_select(out=buf, in_=buf, compare_op=ALU.not_equal, fill=1.0, base=base,
                                   pattern=pattern, channel_multiplier=1).then_inc(pool_set, 1)
                done += 1
            assert done == POOL_SMALL
            for buf, value in later:
                pool.wait_ge(pool_set, done)
                pool.memset(buf, value).then_inc(pool_set, 1)
                done += 1
            assert done == POOL_SET
            for g in range(GROUPS):
                pool.wait_ge(raw_ready, 2 * (g + 1))
                v = raw[g][0:TPT, :, :].rearrange("p h (t n) -> p h t n", n=PARTS)
                pool.affine_select(out=v, in_=v, compare_op=ALU.is_ge, fill=NEG, base=0,
                                   pattern=[[0, GH], [1, TIMES], [0, PARTS]], channel_multiplier=-1).then_inc(raw_masked, 1)
            pool.wait_ge(raw_masked, GROUPS)
            pool.sem_inc(hsum_ready, NH1)
            def unit(r, m):
                pool.wait_ge(h1_ready, r.at(UNITS, m + 1))
                pool.wait_ge(hsum_used, r.at(UNITS, m + 1))
                pool.tensor_tensor(hsum[:, m % NHS, :], h0[:, m % 2, :], h1[:, m % NH1, :],
                                   ALU.add).then_inc(hsum_ready, 1)

            lower_biases(pool, 0)

            def prepare(r, step, a):
                if (step, a) == ("stack", (0, GH - 1)):
                    pool.wait_ge(table_used, HEADS)
                    pool.wait_ge(bias_low[0], 2)
                    v = query_table[:, :, TOK - P:TOK].rearrange("p h (t n) -> p h t n", t=TPT)
                    pool.affine_select(out=v, in_=v, compare_op=ALU.is_ge, fill=NEG, base=0,
                                       pattern=[[0, HEADS], [-PARTS, TPT], [0, PARTS]], channel_multiplier=1).then_inc(setup_done, 1)
                elif (step, a) == ("turn", 1):
                    for a in range(2):
                        pool.wait_ge(w1_high, a + 1)
                        if a:
                            pool.wait_ge(w1_low, a)
                        pool.tensor_tensor(w1_lo[:, 4 * a:4 * a + 4, :], z[:, a, 0:2048].rearrange("p (e f) -> p e f", f=DFF),
                                           w1_hi[:, 4 * a:4 * a + 4, :], ALU.subtract).then_inc(w1_low, 1)

            rounds(pool, lambda r, step, a: None, unit, lambda r, k: None, prepare=prepare)

        @block.scalar
        def _(act):
            act.wait_ge(setup_filled, 1)
            act.copy(b1_col[:, :], narrow[:, 0:EXPERTS * FT]).then_inc(act_set, 1)
            act.wait_ge(setup_filled, 2)
            act.copy(b2_row[:, :], acc[:, 0:C]).then_inc(act_set, 1)
            act.sem_inc(h0_ready, 2)

            def attention(r, step, a):
                if step in WIDE_STEPS:
                    s, _, filled = wide_at(r, step, a)
                    w = wide[s]
                if step == "turn":
                    act.wait_ge(wide_filled[s], filled)
                    act.copy(act_t[:, :], w[:, 0:TOK]).then_inc(wide_free[s], 1)
                elif step in ("query", "key"):
                    n, scale = (0, HD ** -0.5) if step == "query" else (2, 1.0)
                    act.wait_ge(wide_filled[s], filled)
                    act.activation(halves[:, n, :].bitcast(F32R), w[:, 0:TOK], ACT.Copy, scale=scale).then_inc(high_ready, 1)
                elif step == "value":
                    act.wait_ge(wide_filled[s], filled)
                    act.copy(val[:, :, :, 0:HD], w[:, 0:TOK].rearrange("p (i h d) -> p i h d", h=HEADS, d=HD)
                             ).then_inc(wide_free[s], 1)
                elif step == "rows":
                    act.wait_ge(wide_filled[s], filled)
                    act.activation(max_rows[:, 0, :].bitcast(F32R), w[0:GH * TILES, 0:P], ACT.Copy,
                                   scale=-1.0).then_inc(rows_high, 1)
                elif step == "scores":
                    g, hh, part = a
                    act.wait_ge(wide_filled[s], filled)
                    if not (g == 0 and isinstance(r.b, int) and r.b == 0) and hh == 0 and part == 0:
                        n = NARROW["mix", (1 - g, 1)]
                        act.wait_ge(narrow_filled, r.at(NPB, n + 1 - (NPB if g == 0 else 0)))
                    z0, z1 = ((0, 896), (896, 1664), (1664, ZW))[part]
                    act.activation(z[:, hh, z0:z1], w[:, 0:z1 - z0], ACT.Exp).then_inc(wide_free[s], 1)
                elif step == "mix":
                    g, qc = a
                    n = NARROW[step, a]
                    cols = QCOLS if qc == 0 else TOK - QCOLS
                    act.wait_ge(narrow_filled, r.at(NPB, n + 1))
                    if g == 1:
                        act.wait_ge(*taken(r, "divide", 0))
                    act.copy(mixed[:, qc * QCOLS:qc * QCOLS + cols], narrow[:, 0:cols]).then_inc(narrow_free, 1)
                elif step == "gate":
                    act.wait_ge(gate_shifted, r.at(1, 1))
                    act.activation(gate_e[:, :, :], shifted[:, :, :], ACT.Exp).then_inc(gate_exped, 1)
                elif step == "split":
                    act.wait_ge(wide_filled[s], filled)
                    if not (isinstance(r.b, int) and r.b == 0):
                        act.wait_ge(z_filled, r.at(UNITS, (a + 1) * UNITS_PER_CHUNK - UNITS))
                        act.wait_ge(z1_ready, r.at(UNITS, (a + 1) * UNITS_PER_CHUNK - UNITS + 2))
                    act.copy(x0_hi[:, a * CT:(a + 1) * CT], w[:, 0:CT]).then_inc(split_high, 1)
                    act.copy(ratio_b[:, a * CT:(a + 1) * CT], w[:, 512:512 + CT]).then_inc(split_high, 1)

            def unit(r, m):
                j = m % UNITS_PER_CHUNK
                act.wait_ge(hsum_ready, r.at(UNITS, m - 1 + NH1))
                act.wait_ge(z1_ready, r.at(UNITS, m + 1 + 2))
                act.activation(h0[:, m % 2, :], zps[m % 2][:, 0:CT], ACT.Gelu, bias=b1_col[:, j:j + 1]).then_inc(h0_ready, 1)
                act.activation(h1[:, m % NH1, :], h1[:, m % NH1, :], ACT.Gelu, bias=b1_col[:, j:j + 1]).then_inc(h1_ready, 1)

            def prepare(r, step, a):
                if (step, a) == ("value", 0):
                    for g in range(GROUPS):
                        act.wait_ge(raw_masked, g + 1)
                        for row, n in ((0, TPT), (32, PARTS)):
                            act.copy(bias_hi[g][row:row + n], raw[g][row:row + n, :, :]).then_inc(bias_high, 1)
                elif (step, a) == ("turn", 1):
                    act.wait_ge(w1_loaded, 16 * 8)
                    act.wait_ge(bias_placed, 16 * BIAS_DMAS)
                    for a in range(2):
                        act.copy(w1_hi[:, 4 * a:4 * a + 4, :], z[:, a, 0:2048].rearrange("p (e f) -> p e f", f=DFF)).then_inc(w1_high, 1)

            act.wait_ge(act_set, 2)
            rounds(act, attention, unit, lambda r, k: None, prepare=prepare)

        @block.vector
        def _(vec):
            vec.wait_ge(biases_loaded, 16 * 4)
            vec.wait_ge(pool_set, POOL_SMALL)
            for g in range(GROUPS):
                v = raw[g].rearrange("p h (t n) -> p h t n", n=PARTS)
                vec.tensor_copy(v[0:TPT], window(t_stage, (TIMES - 1) * HEADS + g * GH, [[1, GH], [-HEADS, TIMES], [0, PARTS]])
                                ).then_inc(raw_ready, 1)
                vec.tensor_copy(v[32:48], window(p_stage, (PARTS - 1) * HEADS + g * GH, [[1, GH], [0, TIMES], [-HEADS, PARTS]])
                                ).then_inc(raw_ready, 1)

            def fill_rel(h):
                vec.tensor_copy(rel[h % 2][0:TPT, :].rearrange("p (t n) -> p t n", n=PARTS),
                                window(t_stage, h, [[HEADS, TIMES], [0, PARTS]]))
                vec.tensor_copy(rel[h % 2][32:48, :].rearrange("p (t n) -> p t n", n=PARTS),
                                window(p_stage, h, [[0, TIMES], [HEADS, PARTS]])).then_inc(rel_ready, 1)

            def prepare(r, step, a):
                if (step, a) == ("stack", (0, GH - 1)):
                    for h in range(HEADS):
                        vec.wait_ge(table_filled, h + 1)
                        vec.tensor_copy(query_table[:, h, :], wide[h % 2][:, 0:TOK]).then_inc(table_used, 1)
                        if h + 2 < HEADS:
                            fill_rel(h + 2)
                    lower_biases(vec, 1)
                    vec.wait_ge(setup_done, 1)

            vec.tensor_copy(one_hot16, one_hot)
            fill_rel(0)
            fill_rel(1)
            vec.sem_inc(z1_ready, 2)
            vec.sem_inc(out_ready, 1)

            chain = [0]

            def attention(r, step, a):
                def link(ins):
                    chain[0] += 1
                    ins.then_inc(vec_chain, 1)
                    return r.at(VCHAIN, chain[0])

                if step in WIDE_STEPS:
                    s, _, filled = wide_at(r, step, a)
                    w = wide[s]
                if step in ("stats", "scale"):
                    src = x_in if a in (0, (0, 0), (0, 1)) else xs
                if step == "stats":
                    if a == 0:
                        chain[0] = 0
                        vec.wait_ge(x_loaded, r.at(16 * TPT, 16 * TPT))
                    else:
                        vec.wait_ge(*taken(r, "project", 0))
                    for i in range(TILES):
                        ins = vec.bn_stats(stats[:, i, :], src[:, i, :])
                    link(ins)
                elif step == "seed":
                    vec.wait_ge(vec_chain, r.at(VCHAIN, chain[0]))
                    vec.sem_inc(vec_met, 1)
                    for i in range(TILES):
                        ins = vec.bn_aggr(moments[:, i, :], stats[:, i, :])
                    vec.wait_ge(vec_chain, link(ins))
                    vec.wait_ge(vec_chain, link(vec.tensor_scalar(ln_v[:, :], moments[:, :, 1], LN_EPS[a], None, ALU.add)))
                    vec.wait_ge(vec_chain, link(vec.tensor_scalar(ln_i[:, :], ln_v[:, :].bitcast(I32), 1, None,
                                                                  ALU.logical_shift_right)))
                    link(vec.tensor_scalar(ln_y[:, :].bitcast(I32), ln_i[:, :], -1.0, RSQRT_SEED, ALU.mult, ALU.add))
                elif step == "root":
                    vec.wait_ge(vec_chain, r.at(VCHAIN, chain[0]))
                    vec.wait_ge(vec_chain, link(vec.tensor_tensor(ln_t[:, :], ln_y[:, :], ln_y[:, :], ALU.mult)))
                    vec.wait_ge(vec_chain, link(vec.scalar_tensor_tensor(out=ln_t[:, :], in0=ln_t[:, :], scalar=-0.5, in1=ln_v[:, :],
                                                                         op0=ALU.mult, op1=ALU.mult)))
                    link(vec.scalar_tensor_tensor(out=ln_y[:, :], in0=ln_t[:, :], scalar=1.5, in1=ln_y[:, :],
                                                  op0=ALU.add, op1=ALU.mult))
                elif step == "scale":
                    a, half = a
                    vec.wait_ge(vec_chain, r.at(VCHAIN, chain[0]))
                    if a == 0 and not (isinstance(r.b, int) and r.b == 0):
                        n = WIDE["split", 1]
                        vec.wait_ge(wide_filled[n % 2], r.at(WPB, n // 2 + 1 - WPB))
                    for i in range(half * HT, (half + 1) * HT):
                        ins = vec.tensor_scalar(xn[:, i, :], src[:, i, :], moments[:, i, 0:1], ln_y[:, i:i + 1],
                                                ALU.subtract, ALU.mult)
                    ins.then_inc(xn_ready, 1)
                elif step in ("query", "key"):
                    n, scale = (0, HD ** -0.5) if step == "query" else (2, 1.0)
                    vec.wait_ge(high_ready, r.at(2, 1 + n // 2))
                    vec.scalar_tensor_tensor(out=halves[:, n + 1, :].bitcast(F32R), in0=w[:, 0:TOK], scalar=scale,
                                             in1=halves[:, n, :], op0=ALU.mult, op1=ALU.subtract).then_inc(wide_free[s], 1)
                elif step == "maxima":
                    g, hh, part = a
                    h = g * GH + hh
                    vec.wait_ge(wide_filled[s], filled)
                    vec.sem_inc(vec_met, 1)
                    for i, at in (((5, 0), (1, 768)), ((4, 0), (2, 640)), ((3, 0), (0, 512)))[part]:
                        n = (i + 1) * P
                        ins = vec.tensor_tensor_reduce(w[:, at:at + n], w[:, at:at + n],
                                                       query_table[:, h, TOK - n:TOK], 1.0, -3e38, ALU.add, ALU.max,
                                                       maxes[:, hh * TILES + i:hh * TILES + i + 1])
                    ins.then_inc(wide_free[s], 1)
                elif step == "rows":
                    vec.wait_ge(rows_high, r.at(GROUPS, a + 1))
                    vec.scalar_tensor_tensor(out=max_rows[:, 1, :].bitcast(F32R), in0=w[0:GH * TILES, 0:P], scalar=-1.0,
                                             in1=max_rows[:, 0, :], op0=ALU.mult, op1=ALU.subtract).then_inc(wide_free[s], 1)
                elif step == "sums":
                    vec.wait_ge(wide_filled[s], filled)
                    vec.reciprocal(recip[:, :, :], w[:, 0:TILES * GH].rearrange("p (i g) -> p i g", g=GH)).then_inc(wide_free[s], 1)
                elif step == "divide":
                    vec.wait_ge(wide_filled[s], filled)
                    if a == 1:
                        for hh in range(GH):
                            vec.wait_ge(stack_loaded[hh], r.at(2 * 4 * 16, 2 * 4 * 16))
                    vec.tensor_tensor(mixed_n[a][:, 0:TOK], mixed[:, :], w[:, 0:TOK], ALU.mult).then_inc(wide_free[s], 1)
                elif step == "project":
                    vec.wait_ge(wide_filled[s], filled)
                    vec.tensor_tensor(xs[:, :, :], w[:, 0:TOK].rearrange("p (i c) -> p i c", c=C),
                                      x_in[:, :, :], ALU.add).then_inc(wide_free[s], 1)
                elif step == "gate":
                    n = NARROW[step, a]
                    vec.wait_ge(narrow_filled, r.at(NPB, n + 1))
                    vec.sem_inc(vec_met, 1)
                    for i in range(TILES):
                        ins = vec.max(sorted_l[:, i, :], narrow[:, i * EXPERTS:(i + 1) * EXPERTS])
                    ins.then_inc(narrow_free, 1)
                    vec.wait_ge(narrow_free, r.at(NPB, n + 1))
                    vec.tensor_tensor(shifted[:, :, :], sorted_l[:, :, :], window(sorted_l[:, 0, :], 0, [[EXPERTS, TILES], [0, EXPERTS]]),
                                      ALU.subtract).then_inc(gate_shifted, 1)
                elif step == "weigh":
                    vec.wait_ge(gate_exped, r.at(1, 1))
                    vec.wait_ge(vec_chain, link(vec.tensor_reduce(gate_s[:, :, 0], gate_e[:, :, :], AX.X, ALU.add)))
                    vec.wait_ge(vec_chain, link(vec.reciprocal(gate_s[:, :, 1], gate_s[:, :, 0])))
                    vec.wait_ge(vec_chain, link(vec.tensor_tensor(probs[:, :, :], gate_e[:, :, 0:2],
                                                                  window(gate_s[:, 0, :], 1, [[4, TILES], [0, 2]]), ALU.mult)))
                    vec.wait_ge(vec_chain, link(vec.tensor_reduce(gate_s[:, :, 2], probs[:, :, :], AX.X, ALU.add)))
                    vec.wait_ge(vec_chain, link(vec.reciprocal(gate_s[:, :, 3], gate_s[:, :, 2])))
                    vec.wait_ge(vec_chain, link(vec.tensor_tensor(top[:, :, :], probs[:, :, :],
                                                                  window(gate_s[:, 0, :], 3, [[4, TILES], [0, 2]]), ALU.mult)))
                    vec.wait_ge(vec_chain, link(vec.reciprocal(ratio[:, :, 0], top[:, :, 0])))
                    vec.tensor_tensor(ratio[:, :, 1], top[:, :, 1], ratio[:, :, 0], ALU.mult)
                    for i in range(TILES):
                        ins = vec.tensor_scalar(xn[:, i, :], xn[:, i, :], top[:, i, 0:1], None, ALU.mult)
                    ins.then_inc(xn_ready, 1)
                    assert chain[0] == VCHAIN
                elif step == "split":
                    vec.wait_ge(split_high, r.at(4, 2 * a + 2))
                    ins = vec.tensor_tensor(x0_lo[:, a * CT:(a + 1) * CT], w[:, 0:CT], x0_hi[:, a * CT:(a + 1) * CT],
                                            ALU.subtract)
                    ins.then_inc(wide_free[s], 1)
                    if not (isinstance(r.b, int) and r.b == 0) and a == 0:
                        vec.wait_ge(out_ready, r.at(CHUNKS, 1 - CHUNKS + 1))
                    if a == 0:
                        residual(r, 0)
                    elif isinstance(r.b, int) and r.b == 0:
                        residual(r, 1)

            def residual(r, c):
                ts = slice(c * HT, (c + 1) * HT)
                vec.tensor_tensor(res[:, ts, :], xs[:, ts, :], window(b2_row[:, :], 0, [[0, HT], [1, C]]),
                                  ALU.add).then_inc(res_ready, 1)

            def unit(r, m):
                c = m // UNITS_PER_CHUNK
                vec.wait_ge(z_filled, r.at(UNITS, m + 1))
                vec.wait_ge(hsum_ready, r.at(UNITS, m + 1))
                vec.tensor_tensor(h1[:, m % NH1, :], zps[m % 2][:, 0:CT], ratio_b[:, c * CT:(c + 1) * CT],
                                  ALU.mult).then_inc(z1_ready, 1)

            def after(r, k):
                if k % UNITS_PER_CHUNK == UNITS_PER_CHUNK - 1:
                    c = k // UNITS_PER_CHUNK
                    vec.wait_ge(hsum_used, r.at(UNITS, k + 1 + NHS))
                    vec.wait_ge(out_stored, r.at(16 * TPT * CHUNKS, 16 * (TPT * c + 1)))
                    vec.wait_ge(res_ready, r.at(CHUNKS, CHUNKS))
                    vec.tensor_tensor(outt[:, :, :], acc[:, 0:CT].rearrange("p (i c) -> p i c", c=C),
                                      res[:, c * HT:(c + 1) * HT, :], ALU.add).then_inc(out_ready, 1)
                    if c == 1 and not isinstance(r.b, int):
                        vec.wait_ge(out_ready, r.at(CHUNKS, CHUNKS + 1))
                        residual(r, 1)

            rounds(vec, attention, unit, after, last=("stats", "seed", "root", "scale", "rows"), prepare=prepare)

        @block.tensor
        def _(pe):
            pe.wait_ge(pool_set, POOL_SMALL)
            pe.wait_ge(biases_loaded, 16 * 4)
            pe.transpose(narrow[:, 0:EXPERTS * FT], b1_stage, ident[0:32, 0:32]).then_inc(setup_filled, 1)
            pe.matmul(acc[:, 0:C], twos, b2_stage, start=True, stop=True).then_inc(setup_filled, 1)
            pe.wait_ge(weights_loaded, 16 * WEIGHT_DMAS)
            pe.wait_ge(act_set, 2)

            def prepare(r, step, a):
                if (step, a) == ("stack", (0, GH - 1)):
                    pe.wait_ge(*taken(r, "key", 0))
                    pe.wait_ge(*taken(r, "value", 0))
                    for h in range(HEADS):
                        pe.wait_ge(rel_ready, h + 1)
                        if h >= 2:
                            pe.wait_ge(table_used, h - 1)
                        pe.matmul(wide[h % 2][:, 0:512], one_hot16, rel[h % 2][:, 0:512], start=True, stop=True)
                        pe.matmul(wide[h % 2][:, 512:TOK], one_hot16, rel[h % 2][:, 512:TOK], start=True,
                                  stop=True).then_inc(table_filled, 1)
                    pe.wait_ge(table_used, HEADS)
                    pe.wait_ge(setup_done, 1)
                    pe.wait_ge(pool_set, POOL_SET)
                elif (step, a) == PLAN[-1][1:]:
                    pe.wait_ge(w1_low, 2)
                    pe.wait_ge(w2_loaded, 16)

            pe.sem_inc(hsum_used, NHS)

            def attention(r, step, a):
                if step in WIDE_STEPS:
                    s, free, _ = wide_at(r, step, a)
                    w = wide[s]
                    if not (isinstance(free, int) and free <= 0):
                        pe.wait_ge(wide_free[s], free)
                if step in NARROW_STEPS:
                    free = r.at(NPB, NARROW[step, a])
                    if not (isinstance(free, int) and free <= 0):
                        pe.wait_ge(narrow_free, free)
                if step == "turn":
                    pe.wait_ge(xn_ready, r.at(5, 2 * (a + 1)))
                    for i in range(TILES):
                        ins = pe.transpose(w[:, i * P:(i + 1) * P], xn[:, i, :], ident[:, :])
                    ins.then_inc(wide_filled[s], 1)
                elif step in ("query", "key"):
                    pe.wait_ge(*taken(r, "turn", 0))
                    n = 0 if step == "query" else 1
                    pe.matmul(w[:, 0:512], wqkv[:, n, :], act_t[:, 0:512], start=True, stop=True)
                    pe.matmul(w[:, 512:TOK], wqkv[:, n, :], act_t[:, 512:TOK], start=True,
                              stop=True).then_inc(wide_filled[s], 1)
                elif step == "value":
                    for i in range(TILES):
                        ins = pe.matmul(w[:, i * P:(i + 1) * P], act_t[:, i * P:(i + 1) * P], wqkv[:, 2, :],
                                        start=True, stop=True)
                    ins.then_inc(wide_filled[s], 1)
                elif step == "maxima":
                    g, hh, part = a
                    if part == 0:
                        pe.wait_ge(stack_loaded[hh], r.at(2 * 4 * 16, (g + 1) * 4 * 16))
                    for i, k0, k1, at in (((5, 0, 512, 0), (5, 512, 768, 512), (1, 0, 256, 768)),
                                          ((4, 0, 512, 0), (4, 512, 640, 512), (2, 0, 384, 640)),
                                          ((3, 0, 512, 0), (0, 0, 128, 512)))[part]:
                        ins = pe.matmul(w[:, at:at + k1 - k0], qst[0:64, hh, i * P:(i + 1) * P],
                                        kst[0:64, hh, k0:k1], start=True, stop=True)
                    ins.then_inc(wide_filled[s], 1)
                elif step == "rows":
                    pe.wait_ge(*taken(r, "maxima", (a, GH - 1, 2)))
                    pe.transpose(w[0:GH * TILES, 0:P], maxes[:, :], ident[:, :]).then_inc(wide_filled[s], 1)
                elif step == "scores":
                    g, hh, part = a
                    if a == (0, 0, 0) and isinstance(r.b, int):
                        pe.wait_ge(bias_placed, 16 * BIAS_DMAS)
                    if hh == 0 and part == 0:
                        pe.wait_ge(rows_loaded, r.at(2 * 16 * GROUPS, 2 * 16 * (g + 1)))
                    for i, q0, q1, at in (((0, 0, 512, 0), (1, 128, 512, 512)),
                                          ((2, 256, 512, 0), (4, 512, 768, 256), (3, 384, 512, 512), (5, 640, 768, 640)),
                                          ((3, 512, 768, 0), (2, 512, 768, 256), (1, 512, 768, 512), (0, 512, 768, 768)))[part]:
                        pe.matmul(w[:, at:at + q1 - q0], kst[:, hh, i * P:(i + 1) * P], qst[:, hh, q0:q1],
                                  start=True, stop=False)
                        ins = pe.matmul(w[:, at:at + q1 - q0], key_hot[:, g, :], bias_rows[:, hh, q0 - i * P:q1 - i * P],
                                        start=False, stop=True)
                    ins.then_inc(wide_filled[s], 1)
                elif step == "mix":
                    g, qc = a
                    tiles = ((0, 0), (1, 128), (2, 256), (3, 384)) if qc == 0 else \
                        ((0, 0), (1, 0), (2, 0), (3, 0), (4, 0), (5, 128))
                    width = QCOLS if qc == 0 else TOK - QCOLS
                    for n, (i, q0) in enumerate(tiles):
                        for hh in range(GH):
                            if n == 0 and qc == 0:
                                pe.wait_ge(*taken(r, "scores", (g, hh, 2)))
                            at = Z_AT[i, qc]
                            ins = pe.matmul(narrow[32 * hh:32 * hh + 32, q0:width], val[:, i, g * GH + hh, :],
                                            z[:, hh, at:at + width - q0], start=(n == 0), stop=(n == len(tiles) - 1))
                    ins.then_inc(narrow_filled, 1)
                elif step == "sums":
                    pe.wait_ge(narrow_free, r.at(NPB, NARROW["mix", (a, 1)] + 1))
                    for i in range(TILES):
                        ins = pe.matmul(w[:, i * GH:(i + 1) * GH], mixed[:, i * P:(i + 1) * P], pick[:, :], start=True, stop=True)
                    ins.then_inc(wide_filled[s], 1)
                elif step == "divide":
                    pe.wait_ge(*taken(r, "sums", a))
                    for i in range(TILES):
                        for hh in range(GH):
                            ins = pe.matmul(w[32 * hh:32 * hh + 32, i * P:(i + 1) * P], recip[:, i, hh:hh + 1].broadcast_to([P, 32]),
                                            ident[:, :], start=True, stop=True)
                    ins.then_inc(wide_filled[s], 1)
                elif step == "project":
                    pe.wait_ge(*taken(r, "divide", 1))
                    for i in range(TILES):
                        for g in range(GROUPS):
                            ins = pe.matmul(w[:, i * P:(i + 1) * P], mixed_n[g][:, i * P:(i + 1) * P], wo_pad[:, g, :],
                                            start=(g == 0), stop=(g == GROUPS - 1))
                    ins.then_inc(wide_filled[s], 1)
                elif step == "gate":
                    pe.wait_ge(*taken(r, "turn", 1))
                    for i in range(TILES):
                        ins = pe.matmul(narrow[:, i * EXPERTS:(i + 1) * EXPERTS], act_t[:, i * P:(i + 1) * P], wg[:, :],
                                        start=True, stop=True)
                    ins.then_inc(narrow_filled, 1)
                elif step == "split":
                    pe.wait_ge(xn_ready, r.at(5, 5))
                    for n in range(HT):
                        i = a * HT + n
                        pe.transpose(w[:, n * P:(n + 1) * P], xn[:, i, :], ident[:, :])
                        ins = pe.transpose(w[:, 512 + n * P:512 + (n + 1) * P],
                                           ratio[:, i, 1:2].broadcast_to([P, P]), ident[:, :])
                    ins.then_inc(wide_filled[s], 1)

            def unit(r, m):
                c, j = divmod(m, UNITS_PER_CHUNK)
                e, t = divmod(j, FT)
                if j == 0:
                    pe.wait_ge(*taken(r, "split", c))
                pe.wait_ge(h0_ready, r.at(UNITS, m + 1))
                cols = slice(c * CT, (c + 1) * CT)
                zp = zps[m % 2][:, 0:CT]
                hi, lo = w1_hi[:, e, t * P:(t + 1) * P], w1_lo[:, e, t * P:(t + 1) * P]
                pe.matmul(zp, lo, x0_hi[:, cols], start=True, stop=False)
                pe.matmul(zp, hi, x0_lo[:, cols], start=False, stop=False)
                pe.matmul(zp, hi, x0_hi[:, cols], start=False, stop=True).then_inc(z_filled, 1)

            def after(r, k):
                c, j = divmod(k, UNITS_PER_CHUNK)
                pe.wait_ge(hsum_ready, r.at(UNITS, k + 1 + NH1))
                if j == 0:
                    pe.wait_ge(out_ready, r.at(CHUNKS, c + 1))
                for n in range(HT):
                    ins = pe.matmul(acc[:, n * P:(n + 1) * P], hsum[:, k % NHS, n * P:(n + 1) * P], w2[:, j, :],
                                    start=(j == 0 and n == 0), stop=(j == UNITS_PER_CHUNK - 1), skip_group_check=True)
                ins.then_inc(hsum_used, 1)

            rounds(pe, attention, unit, after, prepare=prepare)


WEIGHT_DMAS = 4 + HEADS
POOL_SMALL = 15
POOL_SET = 19
BIAS_DMAS = 8 * GROUPS
_INS = ["x", "L0_conv_Wq", "L0_conv_Wk", "L0_conv_Wv", "L0_conv_Wo", "L0_conv_rel_pos_bias",
        "L0_conv_particle_rel_pos_bias", "L0_ffn_Wg", "L0_ffn_W1", "L0_ffn_b1", "L0_ffn_W2", "L0_ffn_b2"]


def kernel(**inputs):
    import numpy as np
    import concourse.bacc as bacc
    from concourse.bass_utils import run_bass_kernel_spmd

    nc = bacc.Bacc("TRN2", target_bir_lowering=False, num_devices=1)
    arrays, args = {}, []
    for name in _INS:
        a = np.ascontiguousarray(inputs[name])
        arrays[f"in_{name}"] = a
        args.append(nc.dram_tensor(f"in_{name}", a.shape, mybir.dt.from_np(a.dtype), kind="ExternalInput").ap())
    args.append(nc.dram_tensor("out_dram", (BATCHES, PARTS, TIMES, C), F32, kind="ExternalOutput").ap())
    build(nc, *args)
    r = run_bass_kernel_spmd(nc, [arrays], core_ids=[0])
    return r.results[0]["out_dram"]
```
